# Optimizing a Trainium2 kernel written in Bass

```python
import numpy as np
import jax
import jax.numpy as jnp

def _softmax(x, axis=-1):
    return jax.nn.softmax(x, axis=axis)

def _gelu(x):
    return jax.nn.gelu(x, approximate=True)

def _silu(x):
    return jax.nn.silu(x)

def _sigmoid(x):
    return jax.nn.sigmoid(x)

def _layernorm(x, axis=-1, eps=1e-05):
    m = jnp.mean(x, axis=axis, keepdims=True)
    v = jnp.var(x, axis=axis, keepdims=True)
    return (x - m) / jnp.sqrt(v + eps)

def _scatter_add(tgt, idx, src, axis=0):
    return tgt.at[idx].add(src)

def _segment_sum(src, seg, n):
    return jax.ops.segment_sum(src, seg, n)
kernel_name = 'mk_adj_resnorm_d2_adj_r2_0e9a4a'

def setup_inputs(seed: int=0):
    np.random.seed(seed)
    _w = jnp.asarray

    def _rec_inputs():
        import jax
        import jax.numpy as jnp
        _gk = jax.random.key(seed)
        x = -0.0005207 + 1.001 * jax.random.normal(jax.random.fold_in(_gk, 1), (4096, 128), jnp.float32)
        _a = jax.random.bernoulli(jax.random.fold_in(_gk, 2), 0.000488281, (4096, 4096))
        _a = jnp.logical_or(_a, jnp.swapaxes(_a, -1, -2))
        _a = jnp.logical_or(_a, jnp.eye(4096, dtype=bool))
        _af = _a.astype(jnp.float32)
        _af = _af * jax.random.uniform(jax.random.fold_in(_gk, 3), (4096, 4096), jnp.float32, 0.05, 5.41998)
        adj = _af
        return (x, adj)
    x, adj = _rec_inputs()

    def _L0_gnn_setup():
        import jax, jax.numpy as jnp
        import numpy as np
        N = 4096
        C = 128
        key = jax.random.key(seed)
        k1, k2, k3 = jax.random.split(key, 3)
        x = jax.random.normal(k1, (N, C), dtype=jnp.float32)
        evals = jax.random.uniform(k2, (N,), dtype=jnp.float32)
        evecs = jax.random.normal(k3, (N, N), dtype=jnp.float32)
        t = jnp.ones((1,), dtype=jnp.float32)
        return {'x': x, 'evals': evals, 'evecs': evecs, 't': t}
    _L0_gnn_all = _L0_gnn_setup()
    _L0_gnn_in = {k: v for k, v in _L0_gnn_all.items() if k in ('evals', 't')}
    del _L0_gnn_all

    def _L1_gnn_setup():
        import jax, jax.numpy as jnp
        import numpy as np
        NEG_INF = -9000000000000000.0
        NEG_SLOPE = 0.2
        key = jax.random.key(seed)
        k1, k2, k3, k4 = jax.random.split(key, 4)
        N, d_in, d_out = (4096, 128, 128)
        x = jax.random.normal(k1, (N, d_in), dtype=jnp.float32)
        adj = jax.random.randint(k2, (N, N), 0, 2).astype(jnp.float32)
        W = jax.random.normal(k3, (d_in, d_out), dtype=jnp.float32) * (1.0 / np.sqrt(d_in))
        a = jax.random.normal(k4, (2 * d_out,), dtype=jnp.float32) * (1.0 / np.sqrt(2 * d_out))
        return {'x': x, 'adj': adj, 'W': W, 'a': a}
    _L1_gnn_all = _L1_gnn_setup()
    _L1_gnn_in = {k: v for k, v in _L1_gnn_all.items() if k in ('W', 'a')}
    del _L1_gnn_all
    return {'x': x, 'adj': adj, 'L0_gnn_evals': _L0_gnn_in['evals'], 'L0_gnn_t': _L0_gnn_in['t'], 'L1_gnn_W': _L1_gnn_in['W'], 'L1_gnn_a': _L1_gnn_in['a']}

def reference(x, adj, L0_gnn_evals, L0_gnn_t, L1_gnn_W, L1_gnn_a):
    import jax
    import jax.numpy as jnp

    def _L0_gnn_ref(x, evals, evecs, t):
        import jax, jax.numpy as jnp
        import numpy as np
        N = 4096
        C = 128
        t_eff = jnp.clip(t[0], 1e-08, None)
        x_spec = jnp.einsum('nk,nc->kc', evecs, x)
        coefs = jnp.exp(-evals * t_eff)[:, None]
        out = jnp.einsum('nk,kc->nc', evecs, coefs * x_spec)
        return out

    def _L1_gnn_ref(x, adj, W, a):
        import jax, jax.numpy as jnp
        import numpy as np
        NEG_INF = -9000000000000000.0
        NEG_SLOPE = 0.2
        d_out = W.shape[1]
        Wh = x @ W
        e_src = Wh @ a[:d_out]
        e_dst = Wh @ a[d_out:]
        e = jax.nn.leaky_relu(e_src[:, None] + e_dst[None, :], NEG_SLOPE)
        N = Wh.shape[0]
        mask = (adj > 0) | jnp.eye(N, dtype=bool)
        e = jnp.where(mask, e, NEG_INF)
        alpha = jax.nn.softmax(e, axis=1)
        h = alpha @ Wh
        return h
    x = _layernorm(x + _L0_gnn_ref(x, L0_gnn_evals, adj, L0_gnn_t), axis=-1)
    x = _layernorm(x + _L1_gnn_ref(x, adj, L1_gnn_W, L1_gnn_a), axis=-1)
    return x

_drawn_inputs = setup_inputs


def setup_inputs(seed=0):
    import zlib

    import numpy as np

    out = dict(_drawn_inputs(seed))
    spreads = {}
    factors = {}
    for name, (base, spread) in spreads.items():
        noise = np.random.default_rng([zlib.crc32(name.encode()), seed]).standard_normal(out[name].shape)
        drawn = base * np.exp(spread * noise) if base else spread * noise
        out[name] = jnp.asarray(drawn.astype(out[name].dtype))
    for name, factor in factors.items():
        out[name] = (out[name] * factor).astype(out[name].dtype)
    return out
```

```python
from contextlib import ExitStack

import concourse.bass as bass
from concourse import mybir


class StepCount:

    def __init__(self, engine, sem):
        self.engine, self.sem, self.base, self.steps = engine, sem, 0, 0

    def then_wait(self, instruction):
        self.steps += 1
        instruction.then_inc(self.sem, 1)
        self.engine.wait_ge(self.sem, self.base + self.steps)

    def enter_loop(self, turn, per_turn):
        self.outside = self.base + self.steps
        self.per_turn = per_turn
        self.base, self.steps = turn * per_turn + self.outside, 0

    def leave_loop(self, turns):
        assert self.steps == self.per_turn, self.steps
        self.base, self.steps = self.outside + turns * self.per_turn, 0


def build(nc, x, adj, evals, t, W, a, out):
    fp32 = mybir.dt.float32
    int8 = mybir.dt.int8
    ALU = mybir.AluOpType
    ACT = mybir.ActivationFunctionType
    X = mybir.AxisListType.X

    N, C = x.shape
    P = 128
    TILES = N // P
    G = 4
    GW = G * P
    GROUPS = N // GW
    SLOTS = 4
    MASKS = 2
    PIECE = N // SLOTS
    KP = PIECE // P
    BANKS = 8
    LEAD = 3
    HALF = N // 2
    EPS = 1e-5
    SLOPE = 0.2
    MASKED = -128.0
    SCALE = 2.0 ** 46

    mask_dram = nc.dram_tensor("mask_dram", [N, N], int8, kind="Internal").ap()
    x1_dram = nc.dram_tensor("x1_dram", [N, C], fp32, kind="Internal").ap()

    def rows_of_group(ap, g):
        return ap[bass.ds(g * GW, GW), :].rearrange("(u p) c -> p u c", p=P)

    with ExitStack() as ctx:
        def sb(name, shape, dt=fp32):
            return ctx.enter_context(nc.sbuf_tensor(name, shape, dt))

        def sem(name):
            return ctx.enter_context(nc.semaphore(name))

        work = sb("work", [P, 8, N])
        spectrumT = work[:, 4, :]
        filtered = work[:, 5, :].rearrange("p (k c) -> p k c", c=C)
        row_buffer = [[6, 7, 4, 5], [0, 1, 2, 3]]
        mask = sb("mask", [P, MASKS, N], int8)
        values = sb("values", [P, TILES, C])
        e_dst = sb("e_dst", [P, N])
        slope_e_dst = sb("slope_e_dst", [P, N])
        turned = sb("turned", [P, 4, GW])
        x_rows = sb("x_rows", [P, G, C])
        sumT = sb("sumT", [P, GW])
        scratch = sb("scratch", [P, G, C])
        x1_rows = sb("x1_rows", [P, G, C])
        x1T = sb("x1T", [P, GW])
        ident = sb("ident", [P, P])
        not_ident = sb("not_ident", [P, P], int8)
        w_sb = sb("w_sb", [P, C])
        wT = work[:, 7, 0:C]
        a_sb = work[0:2, 7, C:2 * C]
        aT = work[:, 7, 2 * C:2 * C + 2]
        a_wide = work[:, 7, 3 * C:5 * C].rearrange("p (j q) -> p j q", j=2)
        evals_sb = work[0:TILES, 7, 5 * C:6 * C]
        ones = work[0:1, 7, 6 * C:7 * C]
        src_weights = sb("src_weights", [P, C])
        dst_weights = sb("dst_weights", [P, P])
        t_sb = sb("t_sb", [1, 1])
        minus_t = sb("minus_t", [P, 1])
        coefs = sb("coefs", [P, TILES])
        stats = sb("stats", [P, G, 6])
        mean_var = sb("mean_var", [P, G, 2])
        minus_mean, var, rstd, half = (sb(n, [P, G]) for n in ("minus_mean", "var", "rstd", "half"))
        shift_e_src = sb("shift_e_src", [P, TILES])
        part_max = sb("part_max", [P, G, 2])
        minus_max = sb("minus_max", [P, 2, G])
        part_sum = sb("part_sum", [P, 2, G, 2])
        row_sum = sb("row_sum", [P, G])
        one_over_sum = sb("one_over_sum", [P, G])
        e_src_sum = sb("e_src_sum", [P, G])

        ps = ctx.enter_context(nc.psum_tensor("ps", [P, BANKS, 512], fp32))
        ROWS_BANK, PROJ_BANK = 6, 7

        consts_in = sem("consts_in")
        ident_made = sem("ident_made")
        own_gpsimd = sem("own_gpsimd")
        own_vector = sem("own_vector")
        seen_gpsimd = sem("seen_gpsimd")
        seen_vector = sem("seen_vector")
        setup_turned = sem("setup_turned")
        setup_copied = sem("setup_copied")
        setup_weights = sem("setup_weights")
        setup_done = sem("setup_done")
        coefs_made = sem("coefs_made")
        adj_in = [sem(f"adj_in{s}") for s in range(SLOTS)]
        x_in = [sem(f"x_in{s}") for s in range(SLOTS)]
        adj_used = [sem(f"adj_used{s}") for s in range(SLOTS)]
        mask_made = [sem(f"mask_made{s}") for s in range(MASKS)]
        mask_out = [sem(f"mask_out{s}") for s in range(MASKS)]
        spectrum_vector = sem("spectrum_vector")
        spectrum_scalar = sem("spectrum_scalar")
        spectrum_rows = sem("spectrum_rows")
        filtered_made = sem("filtered_made")
        adjT_psum = sem("adjT_psum")
        adjT_ready = sem("adjT_ready")
        adjT_used = sem("adjT_used")
        xg_in = sem("xg_in")
        xg_used = sem("xg_used")
        sumT_ready = sem("sumT_ready")
        rows_psum = sem("rows_psum")
        var_ready = sem("var_ready")
        rstd_ready = sem("rstd_ready")
        x1_ready = sem("x1_ready")
        x1_out = sem("x1_out")
        x1T_psum = sem("x1T_psum")
        x1T_ready = sem("x1T_ready")
        values_psum = sem("values_psum")
        values_ready = sem("values_ready")
        dst_psum = sem("dst_psum")
        dst_ready = sem("dst_ready")
        mask_back = [sem(f"mask_back{s}") for s in range(MASKS)]
        lifted = sem("lifted")
        scores_ready = sem("scores_ready")
        max_ready = sem("max_ready")
        probs_ready = sem("probs_ready")
        probT_psum = sem("probT_psum")
        probT_ready = sem("probT_ready")
        probT_used = sem("probT_used")
        x1g_in = sem("x1g_in")
        x1g_used = sem("x1g_used")
        y_out = sem("y_out")

        block = ctx.enter_context(nc.Block())

        @block.sync
        def _(sp):
            sp.dma_start(w_sb[:, :], W).then_inc(consts_in, 16)
            sp.dma_start(a_sb[:, :], a.rearrange("(j d) -> j d", j=2)).then_inc(consts_in, 16)
            sp.dma_start(evals_sb[:, :], evals.rearrange("(k p) -> k p", p=P)).then_inc(consts_in, 16)
            sp.dma_start(t_sb[:, :], t.rearrange("(a b) -> a b", a=1)).then_inc(consts_in, 16)

            def load_tiles(g, first):
                for s in range(SLOTS):
                    if not first:
                        sp.wait_ge(adj_used[s], g)
                        sp.wait_ge(mask_made[s % MASKS], g * 2 + (s // MASKS - 1))
                    sp.dma_start(work[:, s, :], adj[bass.ds(g * GW + s * P, P), :]).then_inc(adj_in[s], 16)
                    sp.dma_start(x_rows[:, s, :], x[bass.ds(g * GW + s * P, P), :]).then_inc(x_in[s], 16)

            load_tiles(0, True)
            with sp.Fori(1, GROUPS) as g:
                load_tiles(g, False)

            for s in range(SLOTS):
                sp.wait_ge(adj_used[s], GROUPS)
                sp.wait_ge(mask_made[s % MASKS], 2 * GROUPS)

            def load_group(g, first):
                for s in range(SLOTS):
                    if not first:
                        sp.wait_ge(adjT_psum, (g - 1) * TILES + (s + 1) * KP)
                    sp.dma_start(work[:, s, :].rearrange("p (u k) -> p u k", u=G),
                                 rows_of_group(adj, g)[:, :, s * PIECE:(s + 1) * PIECE])\
                        .then_inc(adj_in[s], 16)
                    if s == 0:
                        if not first:
                            sp.wait_ge(xg_used, g)
                        sp.dma_start(x_rows[:, :, :], rows_of_group(x, g)).then_inc(xg_in, 16)

            load_group(0, True)
            with sp.Fori(1, GROUPS) as g:
                load_group(g, False)

            for s in range(MASKS):
                sp.wait_ge(mask_out[s], 2 * 16 * GROUPS)

            def load_mask(g, first):
                for u in range(G):
                    if not first or u >= MASKS:
                        sp.wait_ge(scores_ready, (g * G + u - MASKS) * 2 + 2)
                    sp.dma_start(mask[:, u % MASKS, :], mask_dram[bass.ds(g * GW + u * P, P), :])\
                        .then_inc(mask_back[u % MASKS], 16)

            load_mask(0, True)
            with sp.Fori(1, GROUPS) as g:
                load_mask(g, False)

        @block.gpsimd
        def _(pool):
            nc.gpsimd.memset(ident[:, :], 0.0).then_inc(own_gpsimd, 1)
            nc.gpsimd.memset(not_ident[:, :], 1.0).then_inc(own_gpsimd, 1)
            nc.gpsimd.memset(half[:, :], -0.5).then_inc(own_gpsimd, 1)
            nc.gpsimd.memset(ones[:, :], 1.0).then_inc(own_gpsimd, 1)
            pool.wait_ge(own_gpsimd, 4)
            for m, fill in ((ident, 1.0), (not_ident, 0.0)):
                nc.gpsimd.affine_select(out=m[:, :], in_=m[:, :], compare_op=ALU.not_equal, fill=fill,
                                        base=0, pattern=[[-1, P]], channel_multiplier=1)\
                    .then_inc(ident_made, 1)

            def normalise(turn):
                pool.wait_ge(var_ready, turn + 1)
                nc.gpsimd.tensor_tensor(rstd[:, :], var[:, :], half[:, :], ALU.pow).then_inc(rstd_ready, 1)
                pool.wait_ge(rstd_ready, turn + 1)
                nc.gpsimd.nop().then_inc(seen_gpsimd, 1)
                for u in range(G):
                    last = nc.gpsimd.tensor_scalar(x1_rows[:, u, :], scratch[:, u, :], minus_mean[:, u:u + 1],
                                                   rstd[:, u:u + 1], ALU.add, ALU.mult)
                last.then_inc(x1_ready, 1)
                pool.wait_ge(x1_ready, turn + 1)
                nc.gpsimd.nop().then_inc(seen_gpsimd, 1)

            def keep_x1(g, first):
                if not first:
                    pool.wait_ge(x1_out, g * 16)
                normalise(g)
                pool.dma_start(rows_of_group(x1_dram, g), x1_rows[:, :, :]).then_inc(x1_out, 16)

            keep_x1(0, True)
            with pool.Fori(1, GROUPS) as g:
                keep_x1(g, False)
            pool.wait_ge(x1_out, 16 * GROUPS)

            def write_rows(g, first):
                if not first:
                    pool.wait_ge(x1g_used, g)
                    nc.gpsimd.nop().then_inc(seen_gpsimd, 1)
                pool.dma_start(x_rows[:, :, :], rows_of_group(x1_dram, g)).then_inc(x1g_in, 16)
                if not first:
                    pool.wait_ge(y_out, g * 16)
                normalise(g + GROUPS)
                pool.dma_start(rows_of_group(out, g), x1_rows[:, :, :]).then_inc(y_out, 16)

            write_rows(0, True)
            with pool.Fori(1, GROUPS) as g:
                write_rows(g, False)
            pool.wait_ge(y_out, 16 * GROUPS)

        @block.tensor
        def _(pe):
            pe.wait_ge(ident_made, 2)
            pe.wait_ge(consts_in, 64)
            nc.tensor.transpose(ps[:, 0, 0:TILES], evals_sb[:, :], ident[0:TILES, 0:TILES])
            nc.tensor.transpose(ps[:, 1, 0:C], w_sb[:, :], ident[:, :])
            nc.tensor.transpose(ps[:, 2, 0:2], a_sb[:, :], ident[0:2, 0:2])
            nc.tensor.matmul(ps[:, 3, 0:1], ones[:, :], t_sb[:, :], start=True, stop=True)\
                .then_inc(setup_turned, 1)
            pe.wait_ge(setup_copied, 1)
            nc.tensor.matmul(ps[:, 4, 0:C], a_wide[:, 0, :], wT[:, :], start=True, stop=True)
            nc.tensor.matmul(ps[:, 5, 0:P], wT[:, :], a_wide[:, 1, :], start=True, stop=True)\
                .then_inc(setup_weights, 1)
            pe.wait_ge(setup_done, 1)
            pe.wait_ge(coefs_made, 1)

            def spectral(g, first=False, last=False):
                for s in range(SLOTS):
                    pe.wait_ge(adj_in[s], g * 16 + 16)
                    pe.wait_ge(x_in[s], g * 16 + 16)
                    for b in range(BANKS):
                        mm = nc.tensor.matmul(ps[:, b, :], x_rows[:, s, :], work[:, s, b * 512:(b + 1) * 512],
                                              start=(first and s == 0), stop=(last and s == SLOTS - 1))
                    mm.then_inc(adj_used[s], 1)

            spectral(0, first=True)
            with pe.Fori(1, GROUPS - 1) as g:
                spectral(g)
            spectral(GROUPS - 1, last=True)

            for b in range(BANKS):
                if b % 2 == 0:
                    pe.wait_ge(spectrum_vector, b // 2 + 1)
                else:
                    pe.wait_ge(spectrum_scalar, b // 2 + 1)
                for u in range(G):
                    mm = nc.tensor.transpose(ps[:, b, u * P:(u + 1) * P],
                                             spectrumT[:, b * 512 + u * P:b * 512 + (u + 1) * P], ident[:, :])
                mm.then_inc(spectrum_rows, 1)

            def back_product(g, m, par, first, first_pair):
                pe.wait_ge(adjT_ready, g * TILES + m + 1)
                if m == 0 and not first_pair:
                    pe.wait_ge(sumT_ready, g - 1)
                if first and m % G == 0:
                    pe.wait_ge(filtered_made, max(m // G + 1, 4 + 1))
                nc.tensor.matmul(ps[:, 4 + par, :], filtered[:, m, :], turned[:, m % 4, :],
                                 start=(m == 0), stop=(m == TILES - 1)).then_inc(adjT_used, 1)

            def project(g, k):
                if k == 4:
                    pe.wait_ge(sumT_ready, g + 1)
                    for u in range(G):
                        mm = nc.tensor.transpose(ps[:, ROWS_BANK, u * P:(u + 1) * P],
                                                 sumT[:, u * P:(u + 1) * P], ident[:, :])
                    mm.then_inc(rows_psum, 1)
                if k == 16:
                    pe.wait_ge(x1_ready, g + 1)
                    for u in range(G):
                        mm = nc.tensor.transpose(ps[:, ROWS_BANK, u * P:(u + 1) * P],
                                                 x1_rows[:, u, :], ident[:, :])
                    mm.then_inc(x1T_psum, 1)
                if k == 19:
                    pe.wait_ge(x1T_ready, g + 1)
                    for u in range(G):
                        mm = nc.tensor.matmul(ps[:, PROJ_BANK, u * C:(u + 1) * C],
                                              x1T[:, u * P:(u + 1) * P], w_sb[:, :], start=True, stop=True)
                    mm.then_inc(values_psum, 1)
                if k == 22:
                    pe.wait_ge(values_ready, g + 1)
                    nc.tensor.matmul(ps[:, PROJ_BANK, :], dst_weights[:, :], x1T[:, :],
                                     start=True, stop=True).then_inc(dst_psum, 1)

            def back_group(g, par, first_pair=False):
                first = first_pair and par == 0
                for k in range(TILES):
                    s = k // KP
                    if k % KP == 0:
                        pe.wait_ge(adj_in[s], g * 16 + 16 * (GROUPS + 1))
                    if first and k < LEAD + 1:
                        pe.wait_ge(filtered_made, k + 1)
                    for u in range(G):
                        c = u * PIECE + (k % KP) * P
                        mm = nc.tensor.transpose(ps[:, k % 4, u * P:(u + 1) * P],
                                                 work[:, s, c:c + P], ident[:, :])
                    mm.then_inc(adjT_psum, 1)
                    if k >= LEAD:
                        back_product(g, k - LEAD, par, first, first_pair)
                    elif not first:
                        back_product(g - 1, k - LEAD + TILES, 1 - par, False, False)
                    if not first:
                        project(g - 1, k)

            back_group(0, 0, True)
            back_group(1, 1, True)
            with pe.Fori(1, GROUPS // 2) as j:
                back_group(j * 2, 0)
                back_group(j * 2 + 1, 1)
            for m in range(TILES - LEAD, TILES):
                back_product(GROUPS - 1, m, 1, False, False)
            for k in (4, 16, 19, 22):
                project(GROUPS - 1, k)

            def attend(g, m, par, first_pair):
                pe.wait_ge(probT_ready, g * TILES + m + 1)
                if m == 0 and not first_pair:
                    pe.wait_ge(sumT_ready, g + (GROUPS - 1))
                nc.tensor.matmul(ps[:, 4 + par, :], values[:, m, :], turned[:, m % 4, :],
                                 start=(m == 0), stop=(m == TILES - 1)).then_inc(probT_used, 1)

            def attended_rows(g, first=False):
                pe.wait_ge(sumT_ready, g + (GROUPS + 1))
                if not first:
                    pe.wait_ge(x1g_used, g)
                for u in range(G):
                    mm = nc.tensor.transpose(ps[:, ROWS_BANK, u * P:(u + 1) * P],
                                             sumT[:, u * P:(u + 1) * P], ident[:, :])
                mm.then_inc(rows_psum, 1)

            def attend_group(g, par, first_pair=False):
                first = first_pair and par == 0
                for k in range(TILES):
                    if k == 0:
                        pe.wait_ge(probs_ready, g * 2 * G + 2 * G - 1)
                    if k == TILES // 2:
                        pe.wait_ge(probs_ready, g * 2 * G + 2 * G)
                    for u in range(G):
                        mm = nc.tensor.transpose(ps[:, k % 4, u * P:(u + 1) * P],
                                                 work[:, row_buffer[par][u], k * P:(k + 1) * P], ident[:, :])
                    mm.then_inc(probT_psum, 1)
                    if k >= LEAD:
                        attend(g, k - LEAD, par, first_pair)
                    elif not first:
                        attend(g - 1, k - LEAD + TILES, 1 - par, False)
                    if k == 6 and not first:
                        attended_rows(g - 1, first_pair)

            pe.wait_ge(values_ready, GROUPS)
            attend_group(0, 0, True)
            attend_group(1, 1, True)
            with pe.Fori(1, GROUPS // 2) as j:
                attend_group(j * 2, 0)
                attend_group(j * 2 + 1, 1)
            for m in range(TILES - LEAD, TILES):
                attend(GROUPS - 1, m, 1, False)
            attended_rows(GROUPS - 1)

        @block.scalar
        def _(act):
            act.wait_ge(setup_copied, 1)
            nc.scalar.activation(coefs[:, :], ps[:, 0, 0:TILES], ACT.Exp, scale=minus_t[:, 0:1])\
                .then_inc(coefs_made, 1)

            with act.Fori(0, GROUPS) as g:
                for s in range(SLOTS):
                    act.wait_ge(mask_made[s % MASKS], g * 2 + (s // MASKS + 1))
                    act.dma_start(mask_dram[bass.ds(g * GW + s * P, P), :], mask[:, s % MASKS, :])\
                        .then_inc(mask_out[s % MASKS], 16)

            act.wait_ge(adj_used[SLOTS - 1], GROUPS)
            for b in range(1, BANKS, 2):
                nc.scalar.activation(spectrumT[:, b * 512:(b + 1) * 512], ps[:, b, :], ACT.Copy)\
                    .then_inc(spectrum_scalar, 1)

            def copy_adjT(g, first=False):
                for k in range(TILES):
                    act.wait_ge(adjT_psum, g * TILES + k + 1)
                    if k >= 4 or not first:
                        act.wait_ge(adjT_used, g * TILES + k - 3)
                    nc.scalar.activation(turned[:, k % 4, :], ps[:, k % 4, :], ACT.Copy)\
                        .then_inc(adjT_ready, 1)

            copy_adjT(0, True)
            with act.Fori(1, GROUPS) as g:
                copy_adjT(g)

            def exponent(g, par, u, h):
                act.wait_ge(max_ready, g * G + u + 1)
                rows = work[:, row_buffer[par][u], h * HALF:(h + 1) * HALF]
                nc.scalar.activation(rows, rows, ACT.Exp, bias=minus_max[:, par, u:u + 1],
                                     accum_out=part_sum[:, par, u, h:h + 1]).then_inc(probs_ready, 1)

            def copy_sumT(g, par):
                act.wait_ge(probT_used, g * TILES + TILES)
                nc.scalar.activation(sumT[:, :], ps[:, 4 + par, :], ACT.Copy).then_inc(sumT_ready, 1)

            def window(g, par, first=False, last=False):
                for k in range(TILES):
                    act.wait_ge(probT_psum, g * TILES + k + 1)
                    if k >= 4 or not first:
                        act.wait_ge(probT_used, g * TILES + k - 3)
                    nc.scalar.activation(turned[:, k % 4, :], ps[:, k % 4, :], ACT.Copy)\
                        .then_inc(probT_ready, 1)
                    if k == 0:
                        exponent(g, par, G - 1, 1)
                    if k == 3 and not first:
                        copy_sumT(g - 1, 1 - par)
                    if k in (9, 18, 27) and not last:
                        exponent(g + 1, 1 - par, k // 9 - 1, 0)
                    if k in (10, 19, 28) and not last:
                        exponent(g + 1, 1 - par, k // 9 - 1, 1)
                if not last:
                    exponent(g + 1, 1 - par, G - 1, 0)

            for u in range(G):
                for h in range(2 if u < G - 1 else 1):
                    exponent(0, 0, u, h)
            window(0, 0, first=True)
            window(1, 1)
            with act.Fori(1, GROUPS // 2 - 1) as j:
                window(j * 2, 0)
                window(j * 2 + 1, 1)
            window(GROUPS - 2, 0)
            window(GROUPS - 1, 1, last=True)
            copy_sumT(GROUPS - 1, 1)

        @block.vector
        def _(dve):
            own = StepCount(dve, own_vector)
            dve.wait_ge(setup_turned, 1)
            own.then_wait(nc.vector.tensor_copy(aT[:, :], ps[:, 2, 0:2]))
            nc.vector.tensor_copy(wT[:, :], ps[:, 1, 0:C])
            nc.vector.tensor_scalar(minus_t[:, :], ps[:, 3, 0:1], 1e-8, -1.0, ALU.max, ALU.mult)
            for j in range(2):
                cp = nc.vector.tensor_copy(a_wide[:, j, :], aT[:, j:j + 1].to_broadcast([P, P]))
            cp.then_inc(setup_copied, 1)
            dve.wait_ge(setup_weights, 1)
            nc.vector.tensor_copy(src_weights[:, :], ps[:, 4, 0:C])
            nc.vector.tensor_copy(dst_weights[:, :], ps[:, 5, 0:P]).then_inc(setup_done, 1)
            dve.wait_ge(ident_made, 2)

            def make_masks(g, first):
                for s in range(SLOTS):
                    dve.wait_ge(adj_in[s], g * 16 + 16)
                    if not first or s >= MASKS:
                        dve.wait_ge(mask_out[s % MASKS], g * 32 + s // MASKS * 16)
                    own.then_wait(nc.vector.tensor_scalar(mask[:, s % MASKS, :], work[:, s, :], 0.0, MASKED,
                                                          ALU.is_le, ALU.mult))
                    diagonal = mask[:, s % MASKS, bass.ds(g * GW + s * P, P)]
                    nc.vector.tensor_tensor(diagonal, diagonal, not_ident[:, :], ALU.mult)\
                        .then_inc(mask_made[s % MASKS], 1)

            make_masks(0, True)
            with dve.Fori(1, GROUPS) as g:
                own.enter_loop(g - 1, SLOTS)
                make_masks(g, False)
                own.leave_loop(GROUPS - 1)

            dve.wait_ge(adj_used[SLOTS - 1], GROUPS)
            nc.vector.tensor_copy(spectrumT[:, 0:512], ps[:, 0, :]).then_inc(spectrum_vector, 1)
            for b in range(2, BANKS, 2):
                nc.vector.tensor_copy(spectrumT[:, b * 512:(b + 1) * 512], ps[:, b, :])\
                    .then_inc(spectrum_vector, 1)
            dve.wait_ge(coefs_made, 1)
            for b in range(BANKS):
                dve.wait_ge(spectrum_rows, b + 1)
                nc.vector.tensor_tensor(filtered[:, b * G:(b + 1) * G, :],
                                        ps[:, b, :].rearrange("p (u c) -> p u c", c=C),
                                        coefs[:, b * G:(b + 1) * G].unsqueeze(2).to_broadcast([P, G, C]),
                                        ALU.mult).then_inc(filtered_made, 1)

            def statistics():
                for u in range(G):
                    last = nc.vector.bn_stats(stats[:, u, :], scratch[:, u, :])
                own.then_wait(last)
                nc.vector.nop().then_inc(seen_vector, 1)
                for u in range(G):
                    last = nc.vector.bn_aggr(mean_var[:, u, :], stats[:, u, :])
                own.then_wait(last)
                nc.vector.tensor_scalar(minus_mean[:, :], mean_var[:, :, 0], -1.0, None, ALU.mult)
                nc.vector.tensor_scalar(var[:, :], mean_var[:, :, 1], EPS, None, ALU.add)\
                    .then_inc(var_ready, 1)

            def finish_back(g, par):
                dve.wait_ge(adjT_used, g * TILES + TILES)
                nc.vector.tensor_copy(sumT[:, :], ps[:, 4 + par, :]).then_inc(sumT_ready, 1)
                dve.wait_ge(rows_psum, g + 1)
                dve.wait_ge(xg_in, g * 16 + 16)
                nc.vector.tensor_tensor(scratch[:, :, :], ps[:, ROWS_BANK, :].rearrange("p (u c) -> p u c", c=C),
                                        x_rows[:, :, :], ALU.add).then_inc(xg_used, 1)
                dve.wait_ge(xg_used, g + 1)
                statistics()
                dve.wait_ge(x1_ready, g + 1)
                own.then_wait(nc.vector.tensor_tensor(
                    scratch[:, :, :], x1_rows[:, :, :],
                    src_weights[:, :].unsqueeze(1).to_broadcast([P, G, C]), ALU.mult))
                own.then_wait(nc.vector.reduce_sum(e_src_sum[:, :], scratch[:, :, :], X))
                nc.vector.tensor_scalar(shift_e_src[:, bass.ds(g * G, G)], e_src_sum[:, :],
                                        (SLOPE - 1.0) / SCALE, None, ALU.mult)
                dve.wait_ge(x1T_psum, g + 1)
                nc.vector.tensor_copy(x1T[:, :], ps[:, ROWS_BANK, :]).then_inc(x1T_ready, 1)
                dve.wait_ge(values_psum, g + 1)
                nc.vector.tensor_copy(values[:, bass.ds(g * G, G), :],
                                      ps[:, PROJ_BANK, :].rearrange("p (u c) -> p u c", c=C))\
                    .then_inc(values_ready, 1)
                dve.wait_ge(dst_psum, g + 1)
                nc.vector.tensor_scalar(e_dst[:, bass.ds(g * GW, GW)], ps[:, PROJ_BANK, :],
                                        1.0 / SCALE, None, ALU.mult)
                own.then_wait(nc.vector.tensor_scalar(slope_e_dst[:, bass.ds(g * GW, GW)], ps[:, PROJ_BANK, :],
                                                      SLOPE / SCALE, None, ALU.mult))

            with dve.Fori(0, GROUPS // 2) as j:
                own.enter_loop(j, 2 * 5)
                finish_back(j * 2, 0)
                finish_back(j * 2 + 1, 1)
                own.leave_loop(GROUPS // 2)

            def lift(g, par, u, h):
                cols = slice(h * HALF, (h + 1) * HALF)
                nc.vector.scalar_tensor_tensor(
                    work[:, row_buffer[par][u], cols], slope_e_dst[:, cols],
                    shift_e_src[:, bass.ds(g * G + u, 1)], e_dst[:, cols], ALU.add, ALU.max)\
                    .then_inc(lifted, 1)

            def score(g, par, u, h):
                cols = slice(h * HALF, (h + 1) * HALF)
                rows = work[:, row_buffer[par][u], cols]
                dve.wait_ge(lifted, g * 2 * G + 2 * u + h + 1)
                if h == 0:
                    dve.wait_ge(mask_back[u % MASKS], g * 32 + (u // MASKS * 16 + 16))
                nc.vector.nop().then_inc(seen_vector, 1)
                nc.vector.tensor_tensor_reduce(
                    out=rows, in0=rows, in1=mask[:, u % MASKS, cols],
                    scale=SCALE, scalar=-3.0e38, op0=ALU.add, op1=ALU.max,
                    accum_out=part_max[:, u, h:h + 1]).then_inc(scores_ready, 1)

            def negate_max(g, par, u):
                dve.wait_ge(scores_ready, g * 2 * G + 2 * u + 2)
                nc.vector.tensor_scalar(minus_max[:, par, u:u + 1], part_max[:, u, 0:1],
                                        part_max[:, u, 1:2], -1.0, ALU.max, ALU.mult).then_inc(max_ready, 1)

            def score_group(g, par, first_pair, finish=()):
                finish = iter(finish)
                if not first_pair:
                    dve.wait_ge(probT_psum, (g - 1) * TILES)
                    dve.wait_ge(probs_ready, (g - 1) * 2 * G)
                lift(g, par, 0, 0)
                for u in range(G):
                    lift(g, par, u, 1)
                    score(g, par, u, 0)
                    if u < G - 1:
                        lift(g, par, u + 1, 0)
                    score(g, par, u, 1)
                    next(finish, None)
                    negate_max(g, par, u)
                for _ in finish:
                    pass

            def finish_attention(g, par):
                dve.wait_ge(rows_psum, g + (GROUPS + 1))
                dve.wait_ge(x1g_in, g * 16 + 16)
                dve.wait_ge(x1_ready, g + GROUPS)
                own.then_wait(nc.vector.reduce_sum(row_sum[:, :], part_sum[:, par, :, :], X))
                own.then_wait(nc.vector.reciprocal(one_over_sum[:, :], row_sum[:, :]))
                for u in range(G):
                    last = nc.vector.scalar_tensor_tensor(
                        scratch[:, u, :], ps[:, ROWS_BANK, u * C:(u + 1) * C], one_over_sum[:, u:u + 1],
                        x_rows[:, u, :], ALU.mult, ALU.add)
                last.then_inc(x1g_used, 1)
                dve.wait_ge(x1g_used, g + 1)
                yield
                statistics()

            score_group(0, 0, True)
            score_group(1, 1, True)
            with dve.Fori(1, GROUPS // 2) as j:
                own.enter_loop(j - 1, 2 * 4)
                score_group(j * 2, 0, False, finish_attention(j * 2 - 2, 0))
                score_group(j * 2 + 1, 1, False, finish_attention(j * 2 - 1, 1))
                own.leave_loop(GROUPS // 2 - 1)
            for g in (GROUPS - 2, GROUPS - 1):
                for _ in finish_attention(g, g % 2):
                    pass


_INS = ['x', 'adj', 'L0_gnn_evals', 'L0_gnn_t', 'L1_gnn_W', 'L1_gnn_a']


def kernel(**inputs):
    import numpy as _np
    import concourse.bacc as _bacc
    from concourse import mybir as _mybir
    from concourse.bass_utils import run_bass_kernel_spmd as _run

    nc = _bacc.Bacc("TRN2", target_bir_lowering=False, num_devices=1)
    arrays, args = {}, []
    for name in _INS:
        arr = _np.ascontiguousarray(inputs[name])
        arrays[f"in_{name}"] = arr
        args.append(nc.dram_tensor(f"in_{name}", arr.shape, _mybir.dt.from_np(arr.dtype),
                                   kind="ExternalInput").ap())
    out = nc.dram_tensor("out", inputs['x'].shape, _mybir.dt.float32, kind="ExternalOutput").ap()
    build(nc, *args, out)
    return _run(nc, [arrays], core_ids=[0]).results[0]["out"]
```

```python
from contextlib import ExitStack

import concourse.bass as bass
from concourse import mybir


class StepCount:

    def __init__(self, engine, sem):
        self.engine, self.sem, self.base, self.steps = engine, sem, 0, 0

    def mark(self, instruction):
        self.steps += 1
        instruction.then_inc(self.sem, 1)

    def wait(self):
        self.engine.wait_ge(self.sem, self.base + self.steps)

    def then_wait(self, instruction):
        self.mark(instruction)
        self.wait()

    def enter_loop(self, turn, per_turn):
        self.outside = self.base + self.steps
        self.per_turn = per_turn
        self.base, self.steps = turn * per_turn + self.outside, 0

    def leave_loop(self, turns):
        assert self.steps == self.per_turn, self.steps
        self.base, self.steps = self.outside + turns * self.per_turn, 0


def build(nc, x, adj, evals, t, W, a, out):
    fp32 = mybir.dt.float32
    fp32r = mybir.dt.float32r
    int8 = mybir.dt.int8
    ALU = mybir.AluOpType
    ACT = mybir.ActivationFunctionType
    X = mybir.AxisListType.X

    N, C = x.shape
    P = 128
    TILES = N // P
    G = 4
    GW = G * P
    GROUPS = N // GW
    SLOTS = 4
    MASKS = 2
    PAIR = 2
    PW = PAIR * P
    PAIRS = N // PW
    STEPS = TILES // PAIR
    RING = 4
    PIECE = N // SLOTS
    KP = PIECE // P
    BANKS = 8
    LEAD = 3
    HALF = N // 2
    PARTS = 1 + SLOTS
    EPS = 1e-5
    SLOPE = 0.2
    MASKED = -128.0
    SCALE = 2.0 ** 46

    mask_dram = nc.dram_tensor("mask_dram", [N, N], int8, kind="Internal").ap()
    x1_dram = nc.dram_tensor("x1_dram", [N, C], fp32, kind="Internal").ap()

    def rows_of_group(ap, g):
        return ap[bass.ds(g * GW, GW), :].rearrange("(u p) c -> p u c", p=P)

    def rows_of_pair(ap, n):
        return ap[bass.ds(n * PW, PW), :].rearrange("(u p) c -> p u c", p=P)

    with ExitStack() as ctx:
        def sb(name, shape, dt=fp32):
            return ctx.enter_context(nc.sbuf_tensor(name, shape, dt))

        def sem(name):
            return ctx.enter_context(nc.semaphore(name))

        work = sb("work", [P, SLOTS, N])
        with ExitStack() as products:
            def parts(name, shape):
                return products.enter_context(nc.sbuf_tensor(name, shape, fp32r))

            adjT_high, adjT_low = parts("adjT_high", [P, 4, GW]), parts("adjT_low", [P, 4, GW])
            split_high, split_low = parts("split_high", [P, N]), parts("split_low", [P, N])
        late_rows = sb("late_rows", [P, 4, N])
        spectrumT = late_rows[:, 0, :]
        filtered = late_rows[:, 3, :].rearrange("p (k c) -> p k c", c=C)
        turned = sb("turned", [P, 4, GW])

        def piece_parts(q):
            return split_high[:, q * PIECE:(q + 1) * PIECE], split_low[:, q * PIECE:(q + 1) * PIECE]

        x_high = adjT_high[:, 0, :].rearrange("p (s c) -> p s c", c=C)
        x_low = adjT_low[:, 0, :].rearrange("p (s c) -> p s c", c=C)
        filtered_high = split_high[:, :].rearrange("p (k c) -> p k c", c=C)
        filtered_low = split_low[:, :].rearrange("p (k c) -> p k c", c=C)
        row_buffer = [[work[:, 0, :], work[:, 1, :]], [work[:, 2, :], work[:, 3, :]],
                      [late_rows[:, 0, :], late_rows[:, 1, :]], [late_rows[:, 2, :], late_rows[:, 3, :]]]
        mask = sb("mask", [P, MASKS, N], int8)
        values = sb("values", [P, TILES, C])
        e_dst = sb("e_dst", [P, N])
        slope_e_dst = sb("slope_e_dst", [P, N])
        x_rows = sb("x_rows", [P, G, C])
        sumT = sb("sumT", [P, GW])
        x1_rows = sb("x1_rows", [P, G, C])
        x1T = sumT
        e_src_terms = sumT[:, :].rearrange("p (u c) -> p u c", c=C)
        ident = sb("ident", [P, P])
        not_ident = sb("not_ident", [P, P], int8)
        w_sb = sb("w_sb", [P, C])
        wT = late_rows[:, 3, 0:C]
        a_sb = late_rows[0:2, 3, C:2 * C]
        aT = late_rows[:, 3, 2 * C:2 * C + 2]
        a_wide = late_rows[:, 3, 3 * C:5 * C].rearrange("p (j q) -> p j q", j=2)
        evals_sb = late_rows[0:TILES, 3, 5 * C:6 * C]
        ones = late_rows[0:1, 3, 6 * C:7 * C]
        src_weights = sb("src_weights", [P, C])
        dst_weights = sb("dst_weights", [P, P])
        t_sb = sb("t_sb", [1, 1])
        minus_t = sb("minus_t", [P, 1])
        coefs = sb("coefs", [P, TILES])
        stats = sb("stats", [P, G, 6])
        mean_var = sb("mean_var", [P, G, 2])
        minus_mean, var, rstd, half = (sb(n, [P, G]) for n in ("minus_mean", "var", "rstd", "half"))
        shift_e_src = sb("shift_e_src", [P, TILES])
        part_max = sb("part_max", [P, PAIR, 2])
        minus_max = sb("minus_max", [P, RING, PAIR])
        part_sum = sb("part_sum", [P, RING, PAIR, 2])
        row_sum = sb("row_sum", [P, PAIR])
        one_over_sum = sb("one_over_sum", [P, PAIR])
        e_src_sum = sb("e_src_sum", [P, G])

        ps = ctx.enter_context(nc.psum_tensor("ps", [P, BANKS, 512], fp32))
        ROWS_BANK, PROJ_BANK = 6, 7

        consts_in = sem("consts_in")
        ident_made = sem("ident_made")
        own_gpsimd = sem("own_gpsimd")
        own_vector = sem("own_vector")
        seen_gpsimd = sem("seen_gpsimd")
        seen_vector = sem("seen_vector")
        seen_sync = sem("seen_sync")
        setup_turned = sem("setup_turned")
        setup_copied = sem("setup_copied")
        setup_weights = sem("setup_weights")
        setup_done = sem("setup_done")
        coefs_made = sem("coefs_made")
        adj_in = [sem(f"adj_in{s}") for s in range(SLOTS)]
        x_in = [sem(f"x_in{s}") for s in range(SLOTS)]
        high_made = sem("high_made")
        low_made = sem("low_made")
        pieces_used = sem("pieces_used")
        mask_made = [sem(f"mask_made{s}") for s in range(MASKS)]
        mask_out = [sem(f"mask_out{s}") for s in range(MASKS)]
        spectrum_vector = sem("spectrum_vector")
        spectrum_scalar = sem("spectrum_scalar")
        spectrum_rows = sem("spectrum_rows")
        filtered_made = sem("filtered_made")
        filtered_high_made = sem("filtered_high_made")
        filtered_low_made = sem("filtered_low_made")
        adjT_psum = sem("adjT_psum")
        adjT_high_made = sem("adjT_high_made")
        adjT_low_made = sem("adjT_low_made")
        adjT_used = sem("adjT_used")
        xg_in = sem("xg_in")
        rows_added = sem("rows_added")
        sumT_ready = sem("sumT_ready")
        rows_psum = sem("rows_psum")
        var_ready = sem("var_ready")
        rstd_ready = sem("rstd_ready")
        x1_ready = sem("x1_ready")
        x1_out = sem("x1_out")
        x1T_psum = sem("x1T_psum")
        x1T_ready = sem("x1T_ready")
        values_psum = sem("values_psum")
        values_ready = sem("values_ready")
        dst_psum = sem("dst_psum")
        dst_ready = sem("dst_ready")
        mask_back = [sem(f"mask_back{s}") for s in range(MASKS)]
        opened = sem("opened")
        lifted = sem("lifted")
        scores_ready = sem("scores_ready")
        max_ready = sem("max_ready")
        probs_ready = sem("probs_ready")
        probT_psum = sem("probT_psum")
        probT_ready = sem("probT_ready")
        probT_used = sem("probT_used")
        x1g_in = sem("x1g_in")
        x1g_added = sem("x1g_added")
        y_out = sem("y_out")

        block = ctx.enter_context(nc.Block())

        @block.sync
        def _(sp):
            sp.dma_start(w_sb[:, :], W).then_inc(consts_in, 16)
            sp.dma_start(a_sb[:, :], a.rearrange("(j d) -> j d", j=2)).then_inc(consts_in, 16)
            sp.dma_start(evals_sb[:, :], evals.rearrange("(k p) -> k p", p=P)).then_inc(consts_in, 16)
            sp.dma_start(t_sb[:, :], t.rearrange("(a b) -> a b", a=1)).then_inc(consts_in, 16)

            def load_tiles(g, first):
                for s in range(SLOTS):
                    if not first:
                        sp.wait_ge(low_made, g * (SLOTS * PARTS) + PARTS * (s + 1 - SLOTS))
                    sp.dma_start(work[:, s, :], adj[bass.ds(g * GW + s * P, P), :]).then_inc(adj_in[s], 16)
                    sp.dma_start(x_rows[:, s, :], x[bass.ds(g * GW + s * P, P), :]).then_inc(x_in[s], 16)

            load_tiles(0, True)
            with sp.Fori(1, GROUPS) as g:
                load_tiles(g, False)

            def load_piece(g, s):
                sp.dma_start(work[:, s, :].rearrange("p (u k) -> p u k", u=G),
                             rows_of_group(adj, g)[:, :, s * PIECE:(s + 1) * PIECE])\
                    .then_inc(adj_in[s], 16)

            def write_mask(g, s):
                sp.wait_ge(mask_made[s % MASKS], g * 2 + (s // MASKS + 1))
                nc.sync.nop().then_inc(seen_sync, 1)
                sp.dma_start(rows_of_group(mask_dram, g)[:, :, s * PIECE:(s + 1) * PIECE],
                             mask[:, s % MASKS, :].rearrange("p (u k) -> p u k", u=G))\
                    .then_inc(mask_out[s % MASKS], 16)

            def load_x(g):
                sp.dma_start(x_rows[:, :, :], rows_of_group(x, g)).then_inc(xg_in, 16)

            for s in range(SLOTS):
                sp.wait_ge(low_made, PARTS * (TILES - SLOTS + s + 1))
                load_piece(0, s)
            load_x(0)

            def pass_group(g, first):
                for s in range(SLOTS):
                    sp.wait_ge(adjT_psum, g * TILES + (s + 1) * KP)
                    nc.sync.nop().then_inc(seen_sync, 1)
                    write_mask(g, s)
                    load_piece(g + 1, s)
                    if s == 1 and not first:
                        sp.wait_ge(x1_ready, g)
                        nc.sync.nop().then_inc(seen_sync, 1)
                        load_x(g)

            pass_group(0, True)
            with sp.Fori(1, GROUPS - 1) as g:
                pass_group(g, False)
            for s in range(SLOTS):
                write_mask(GROUPS - 1, s)
                if s == 1:
                    sp.wait_ge(x1_ready, GROUPS - 1)
                    load_x(GROUPS - 1)

            for s in range(MASKS):
                sp.wait_ge(mask_out[s], 2 * 16 * GROUPS)

            def load_mask(n, first):
                for u in range(PAIR):
                    if not first:
                        sp.wait_ge(scores_ready, n * 2 * PAIR + (2 * u + 2 - 2 * PAIR))
                    sp.dma_start(mask[:, u, :], mask_dram[bass.ds(n * PW + u * P, P), :])\
                        .then_inc(mask_back[u], 16)

            load_mask(0, True)
            with sp.Fori(1, PAIRS) as n:
                load_mask(n, False)

        @block.gpsimd
        def _(pool):
            nc.gpsimd.memset(ident[:, :], 0.0).then_inc(own_gpsimd, 1)
            nc.gpsimd.memset(not_ident[:, :], 1.0).then_inc(own_gpsimd, 1)
            nc.gpsimd.memset(half[:, :], -0.5).then_inc(own_gpsimd, 1)
            nc.gpsimd.memset(ones[:, :], 1.0).then_inc(own_gpsimd, 1)
            pool.wait_ge(own_gpsimd, 4)
            for m, fill in ((ident, 1.0), (not_ident, 0.0)):
                nc.gpsimd.affine_select(out=m[:, :], in_=m[:, :], compare_op=ALU.not_equal, fill=fill,
                                        base=0, pattern=[[-1, P]], channel_multiplier=1)\
                    .then_inc(ident_made, 1)

            def normalise(turn, tiles):
                pool.wait_ge(var_ready, turn + 1)
                nc.gpsimd.tensor_tensor(rstd[:, :tiles], var[:, :tiles], half[:, :tiles], ALU.pow)\
                    .then_inc(rstd_ready, 1)
                pool.wait_ge(rstd_ready, turn + 1)
                nc.gpsimd.nop().then_inc(seen_gpsimd, 1)
                for u in range(tiles):
                    last = nc.gpsimd.tensor_scalar(x1_rows[:, u, :], x_rows[:, u, :], minus_mean[:, u:u + 1],
                                                   rstd[:, u:u + 1], ALU.add, ALU.mult)
                last.then_inc(x1_ready, 1)
                pool.wait_ge(x1_ready, turn + 1)
                nc.gpsimd.nop().then_inc(seen_gpsimd, 1)

            def keep_x1(g, first):
                if not first:
                    pool.wait_ge(x1_out, g * 16)
                normalise(g, G)
                pool.dma_start(rows_of_group(x1_dram, g), x1_rows[:, :, :]).then_inc(x1_out, 16)

            keep_x1(0, True)
            with pool.Fori(1, GROUPS) as g:
                keep_x1(g, False)
            pool.wait_ge(x1_out, 16 * GROUPS)

            def write_rows(n, first):
                pool.dma_start(x_rows[:, :PAIR, :], rows_of_pair(x1_dram, n)).then_inc(x1g_in, 16)
                if not first:
                    pool.wait_ge(y_out, n * 16)
                normalise(n + GROUPS, PAIR)
                pool.dma_start(rows_of_pair(out, n), x1_rows[:, :PAIR, :]).then_inc(y_out, 16)

            write_rows(0, True)
            with pool.Fori(1, PAIRS) as n:
                write_rows(n, False)
            pool.wait_ge(y_out, 16 * PAIRS)

        @block.tensor
        def _(pe):
            pe.wait_ge(ident_made, 2)
            pe.wait_ge(consts_in, 64)
            nc.tensor.transpose(ps[:, 0, 0:TILES], evals_sb[:, :], ident[0:TILES, 0:TILES])
            nc.tensor.transpose(ps[:, 1, 0:C], w_sb[:, :], ident[:, :])
            nc.tensor.transpose(ps[:, 2, 0:2], a_sb[:, :], ident[0:2, 0:2])
            nc.tensor.matmul(ps[:, 3, 0:1], ones[:, :], t_sb[:, :], start=True, stop=True)\
                .then_inc(setup_turned, 1)
            pe.wait_ge(setup_copied, 1)
            nc.tensor.matmul(ps[:, 4, 0:C], a_wide[:, 0, :], wT[:, :], start=True, stop=True)
            nc.tensor.matmul(ps[:, 5, 0:P], wT[:, :], a_wide[:, 1, :], start=True, stop=True)\
                .then_inc(setup_weights, 1)
            pe.wait_ge(setup_done, 1)
            pe.wait_ge(coefs_made, 1)

            def spectral(g, first=False, last=False):
                for s in range(SLOTS):
                    for q in range(SLOTS):
                        pe.wait_ge(low_made, g * (SLOTS * PARTS) + s * PARTS + q + 2)
                        high, low = piece_parts(q)
                        for b in range(2):
                            cols = slice(b * 512, (b + 1) * 512)
                            for n, (xs, adjs) in enumerate(((x_high, high), (x_low, high), (x_high, low))):
                                mm = nc.tensor.matmul(ps[:, 2 * q + b, :], xs[:, s, :], adjs[:, cols],
                                                      start=(first and s == 0 and n == 0),
                                                      stop=(last and s == SLOTS - 1 and n == 2))
                        mm.then_inc(pieces_used, 1)

            spectral(0, first=True)
            with pe.Fori(1, GROUPS - 1) as g:
                spectral(g)
            spectral(GROUPS - 1, last=True)

            for b in range(BANKS):
                if b % 2 == 0:
                    pe.wait_ge(spectrum_vector, b // 2 + 1)
                else:
                    pe.wait_ge(spectrum_scalar, b // 2 + 1)
                for u in range(G):
                    mm = nc.tensor.transpose(ps[:, b, u * P:(u + 1) * P],
                                             spectrumT[:, b * 512 + u * P:b * 512 + (u + 1) * P], ident[:, :])
                mm.then_inc(spectrum_rows, 1)

            def back_product(g, m, par, first, first_pair):
                pe.wait_ge(adjT_low_made, g * TILES + m + 1)
                if m == 0 and not first_pair:
                    pe.wait_ge(sumT_ready, g - 1)
                if first and m == 0:
                    pe.wait_ge(filtered_made, 4 + 1)
                if first and m % G == 0:
                    pe.wait_ge(filtered_low_made, m // G + 1)
                for n, (ys, adjs) in enumerate(((filtered_high, adjT_high[:, m % 4, :]),
                                                (filtered_low, adjT_high[:, m % 4, :]),
                                                (filtered_high, adjT_low[:, m % 4, :]))):
                    mm = nc.tensor.matmul(ps[:, 4 + par, :], ys[:, m, :], adjs,
                                          start=(m == 0 and n == 0), stop=(m == TILES - 1 and n == 2))
                mm.then_inc(adjT_used, 1)

            def project(g, k):
                if k == 4:
                    pe.wait_ge(sumT_ready, g + 1)
                    for u in range(G):
                        mm = nc.tensor.transpose(ps[:, ROWS_BANK, u * P:(u + 1) * P],
                                                 sumT[:, u * P:(u + 1) * P], ident[:, :])
                    mm.then_inc(rows_psum, 1)
                if k == 16:
                    pe.wait_ge(x1_ready, g + 1)
                    for u in range(G):
                        mm = nc.tensor.transpose(ps[:, ROWS_BANK, u * P:(u + 1) * P],
                                                 x1_rows[:, u, :], ident[:, :])
                    mm.then_inc(x1T_psum, 1)
                if k == 19:
                    pe.wait_ge(x1T_ready, g + 1)
                    nc.tensor.matmul(ps[:, PROJ_BANK, :], dst_weights[:, :], x1T[:, :],
                                     start=True, stop=True).then_inc(dst_psum, 1)
                if k == 22:
                    pe.wait_ge(dst_ready, g + 1)
                    for u in range(G):
                        mm = nc.tensor.matmul(ps[:, PROJ_BANK, u * C:(u + 1) * C],
                                              x1T[:, u * P:(u + 1) * P], w_sb[:, :], start=True, stop=True)
                    mm.then_inc(values_psum, 1)

            def back_group(g, par, first_pair=False):
                first = first_pair and par == 0
                for k in range(TILES):
                    s = k // KP
                    if k % KP == 0:
                        pe.wait_ge(adj_in[s], g * 16 + 16 * (GROUPS + 1))
                    if first and k < LEAD + 1:
                        pe.wait_ge(filtered_made, k + 1)
                    for u in range(G):
                        c = u * PIECE + (k % KP) * P
                        mm = nc.tensor.transpose(ps[:, k % 4, u * P:(u + 1) * P],
                                                 work[:, s, c:c + P], ident[:, :])
                    mm.then_inc(adjT_psum, 1)
                    if k >= LEAD:
                        back_product(g, k - LEAD, par, first, first_pair)
                    elif not first:
                        back_product(g - 1, k - LEAD + TILES, 1 - par, False, False)
                    if not first:
                        project(g - 1, k)

            back_group(0, 0, True)
            back_group(1, 1, True)
            with pe.Fori(1, GROUPS // 2) as j:
                back_group(j * 2, 0)
                back_group(j * 2 + 1, 1)
            for m in range(TILES - LEAD, TILES):
                back_product(GROUPS - 1, m, 1, False, False)
            for k in (4, 16, 19, 22):
                project(GROUPS - 1, k)

            def attend(n, slot, k, first_pairs=False, first_group=False):
                pe.wait_ge(probT_ready, n * STEPS + k + 1)
                if first_group and k == (TILES - G) // 2:
                    pe.wait_ge(values_ready, GROUPS)
                if k == 0 and not first_pairs:
                    pe.wait_ge(sumT_ready, n + (GROUPS - 1))
                for i in range(2):
                    mm = nc.tensor.matmul(ps[:, 4 + slot % 2, :PW], values[:, 2 * k + i, :],
                                          turned[:, k % 4, i * PW:(i + 1) * PW],
                                          start=(k == 0 and i == 0), stop=(k == STEPS - 1 and i == 1))
                mm.then_inc(probT_used, 1)

            def attended_rows(n, first=False):
                pe.wait_ge(sumT_ready, n + (GROUPS + 1))
                if not first:
                    pe.wait_ge(x1g_added, n)
                for u in range(PAIR):
                    mm = nc.tensor.transpose(ps[:, ROWS_BANK, u * P:(u + 1) * P],
                                             sumT[:, u * P:(u + 1) * P], ident[:, :])
                mm.then_inc(rows_psum, 1)

            def attend_pair(n, slot, first=False, second=False):
                for k in range(STEPS):
                    if k == 0:
                        pe.wait_ge(probs_ready, n * 2 * PAIR + 2 * PAIR - 1)
                    if k == STEPS // 2:
                        pe.wait_ge(probs_ready, n * 2 * PAIR + 2 * PAIR)
                    for i in range(2):
                        for u in range(PAIR):
                            m = 2 * k + i
                            mm = nc.tensor.transpose(ps[:, k % 4, i * PW + u * P:i * PW + (u + 1) * P],
                                                     row_buffer[slot][u][:, m * P:(m + 1) * P], ident[:, :])
                    mm.then_inc(probT_psum, 1)
                    if k >= LEAD:
                        attend(n, slot, k - LEAD, first or second, first)
                    elif not first:
                        attend(n - 1, (slot - 1) % RING, k - LEAD + STEPS, second)
                    if k == 5 and not first:
                        attended_rows(n - 1, second)

            pe.wait_ge(values_ready, GROUPS - 1)
            for n in range(RING):
                attend_pair(n, n, first=(n == 0), second=(n == 1))
            with pe.Fori(1, PAIRS // RING) as j:
                for slot in range(RING):
                    attend_pair(j * RING + slot, slot)
            for k in range(STEPS - LEAD, STEPS):
                attend(PAIRS - 1, RING - 1, k)
            attended_rows(PAIRS - 1)

        @block.scalar
        def _(act):
            act.wait_ge(setup_copied, 1)
            nc.scalar.activation(coefs[:, :], ps[:, 0, 0:TILES], ACT.Exp, scale=minus_t[:, 0:1])\
                .then_inc(coefs_made, 1)

            def split_high_parts(g, first):
                for s in range(SLOTS):
                    act.wait_ge(x_in[s], g * 16 + 16)
                    if not first:
                        act.wait_ge(pieces_used, g * (SLOTS * SLOTS) + (s + 1 - SLOTS) * SLOTS)
                    nc.scalar.activation(x_high[:, s, :], x_rows[:, s, :], ACT.Copy).then_inc(high_made, 1)
                    act.wait_ge(adj_in[s], g * 16 + 16)
                    for q in range(SLOTS):
                        if not first or s > 0:
                            act.wait_ge(pieces_used, g * (SLOTS * SLOTS) + (s - 1) * SLOTS + q + 1)
                        nc.scalar.activation(piece_parts(q)[0], work[:, s, q * PIECE:(q + 1) * PIECE], ACT.Copy)\
                            .then_inc(high_made, 1)

            split_high_parts(0, True)
            with act.Fori(1, GROUPS) as g:
                split_high_parts(g, False)

            act.wait_ge(pieces_used, TILES * SLOTS)
            for b in range(1, BANKS, 2):
                nc.scalar.activation(spectrumT[:, b * 512:(b + 1) * 512], ps[:, b, :], ACT.Copy)\
                    .then_inc(spectrum_scalar, 1)

            def split_filtered(b):
                act.wait_ge(filtered_made, b + 1)
                nc.scalar.activation(filtered_high[:, b * G:(b + 1) * G, :], filtered[:, b * G:(b + 1) * G, :],
                                     ACT.Copy).then_inc(filtered_high_made, 1)

            split_filtered(0)

            def split_adjT(g, first=False):
                for k in range(TILES):
                    act.wait_ge(adjT_psum, g * TILES + k + 1)
                    if first and k == 0:
                        act.wait_ge(spectrum_rows, BANKS)
                    if k >= 4 or not first:
                        act.wait_ge(adjT_used, g * TILES + k - 3)
                    nc.scalar.activation(adjT_high[:, k % 4, :], ps[:, k % 4, :], ACT.Copy)\
                        .then_inc(adjT_high_made, 1)
                    if first and k % 4 == 1 and k < TILES - 4:
                        split_filtered(k // 4 + 1)

            split_adjT(0, True)
            with act.Fori(1, GROUPS) as g:
                split_adjT(g)

            def exponent(n, slot, u, h):
                act.wait_ge(max_ready, n * PAIR + u + 1)
                rows = row_buffer[slot][u][:, h * HALF:(h + 1) * HALF]
                nc.scalar.activation(rows, rows, ACT.Exp, bias=minus_max[:, slot, u:u + 1],
                                     accum_out=part_sum[:, slot, u, h:h + 1]).then_inc(probs_ready, 1)

            def copy_sumT(n, slot):
                act.wait_ge(probT_used, n * STEPS + STEPS)
                nc.scalar.activation(sumT[:, :PW], ps[:, 4 + slot % 2, :PW], ACT.Copy).then_inc(sumT_ready, 1)

            def window(n, slot, first=False, last=False):
                after = (slot + 1) % RING
                when = (9, 11, 15) if first else (5, 9, 13)
                for k in range(STEPS):
                    act.wait_ge(probT_psum, n * STEPS + k + 1)
                    if k >= 4 or not first:
                        act.wait_ge(probT_used, n * STEPS + k - 3)
                    nc.scalar.activation(turned[:, k % 4, :], ps[:, k % 4, :], ACT.Copy)\
                        .then_inc(probT_ready, 1)
                    if k == 1:
                        exponent(n, slot, PAIR - 1, 1)
                    if k == 3 and not first:
                        copy_sumT(n - 1, (slot - 1) % RING)
                    if k in when and not last:
                        exponent(n + 1, after, *((0, 0), (0, 1), (1, 0))[when.index(k)])

            for u, h in ((0, 0), (0, 1), (1, 0)):
                exponent(0, 0, u, h)
            for n in range(RING):
                window(n, n, first=(n == 0))
            with act.Fori(1, PAIRS // RING - 1) as j:
                for slot in range(RING):
                    window(j * RING + slot, slot)
            for slot in range(RING):
                window(PAIRS - RING + slot, slot, last=(slot == RING - 1))
            copy_sumT(PAIRS - 1, RING - 1)

        @block.vector
        def _(dve):
            own = StepCount(dve, own_vector)
            dve.wait_ge(setup_turned, 1)
            own.then_wait(nc.vector.tensor_copy(aT[:, :], ps[:, 2, 0:2]))
            nc.vector.tensor_copy(wT[:, :], ps[:, 1, 0:C])
            nc.vector.tensor_scalar(minus_t[:, :], ps[:, 3, 0:1], 1e-8, -1.0, ALU.max, ALU.mult)
            for j in range(2):
                cp = nc.vector.tensor_copy(a_wide[:, j, :], aT[:, j:j + 1].to_broadcast([P, P]))
            cp.then_inc(setup_copied, 1)
            dve.wait_ge(setup_weights, 1)
            nc.vector.tensor_copy(src_weights[:, :], ps[:, 4, 0:C])
            nc.vector.tensor_copy(dst_weights[:, :], ps[:, 5, 0:P]).then_inc(setup_done, 1)
            dve.wait_ge(ident_made, 2)

            def low_part(low, whole, high):
                return nc.vector.tensor_tensor(low, whole, high.bitcast(fp32), ALU.subtract)

            def split_low_parts(g):
                for s in range(SLOTS):
                    dve.wait_ge(high_made, g * (SLOTS * PARTS) + s * PARTS + 1)
                    low_part(x_low[:, s, :], x_rows[:, s, :], x_high[:, s, :]).then_inc(low_made, 1)
                    for q in range(SLOTS):
                        dve.wait_ge(high_made, g * (SLOTS * PARTS) + s * PARTS + q + 2)
                        high, low = piece_parts(q)
                        low_part(low, work[:, s, q * PIECE:(q + 1) * PIECE], high).then_inc(low_made, 1)

            with dve.Fori(0, GROUPS) as g:
                split_low_parts(g)

            dve.wait_ge(pieces_used, TILES * SLOTS)
            for b in range(0, BANKS, 2):
                nc.vector.tensor_copy(spectrumT[:, b * 512:(b + 1) * 512], ps[:, b, :])\
                    .then_inc(spectrum_vector, 1)

            def filter_bank(b):
                dve.wait_ge(spectrum_rows, b + 1)
                nc.vector.tensor_tensor(filtered[:, b * G:(b + 1) * G, :],
                                        ps[:, b, :].rearrange("p (u c) -> p u c", c=C),
                                        coefs[:, b * G:(b + 1) * G].unsqueeze(2).to_broadcast([P, G, C]),
                                        ALU.mult).then_inc(filtered_made, 1)

            def filtered_low_part(b):
                dve.wait_ge(filtered_high_made, b + 1)
                k = slice(b * G, (b + 1) * G)
                low_part(filtered_low[:, k, :], filtered[:, k, :], filtered_high[:, k, :])\
                    .then_inc(filtered_low_made, 1)

            dve.wait_ge(coefs_made, 1)
            for b in range(5):
                filter_bank(b)
            filtered_low_part(0)

            def statistics(tiles):
                for u in range(tiles):
                    last = nc.vector.bn_stats(stats[:, u, :], x_rows[:, u, :])
                own.mark(last)
                yield
                own.wait()
                nc.vector.nop().then_inc(seen_vector, 1)
                for u in range(tiles):
                    last = nc.vector.bn_aggr(mean_var[:, u, :], stats[:, u, :])
                own.then_wait(last)
                nc.vector.tensor_scalar(minus_mean[:, :tiles], mean_var[:, :tiles, 0], -1.0, None, ALU.mult)
                nc.vector.tensor_scalar(var[:, :tiles], mean_var[:, :tiles, 1], EPS, None, ALU.add)\
                    .then_inc(var_ready, 1)

            def finish_back(g, par):
                dve.wait_ge(adjT_used, g * TILES + TILES)
                nc.vector.tensor_copy(sumT[:, :], ps[:, 4 + par, :]).then_inc(sumT_ready, 1)
                yield
                dve.wait_ge(rows_psum, g + 1)
                dve.wait_ge(xg_in, g * 16 + 16)
                nc.vector.tensor_tensor(x_rows[:, :, :], ps[:, ROWS_BANK, :].rearrange("p (u c) -> p u c", c=C),
                                        x_rows[:, :, :], ALU.add).then_inc(rows_added, 1)
                yield
                dve.wait_ge(rows_added, g + 1)
                yield from statistics(G)
                yield
                dve.wait_ge(x1T_psum, g + 1)
                nc.vector.tensor_copy(x1T[:, :], ps[:, ROWS_BANK, :]).then_inc(x1T_ready, 1)
                yield
                dve.wait_ge(dst_psum, g + 1)
                nc.vector.tensor_scalar(e_dst[:, bass.ds(g * GW, GW)], ps[:, PROJ_BANK, :],
                                        1.0 / SCALE, None, ALU.mult)
                nc.vector.tensor_scalar(slope_e_dst[:, bass.ds(g * GW, GW)], ps[:, PROJ_BANK, :],
                                        SLOPE / SCALE, None, ALU.mult).then_inc(dst_ready, 1)
                yield
                dve.wait_ge(values_psum, g + 1)
                own.mark(nc.vector.tensor_tensor(
                    e_src_terms, x1_rows[:, :, :],
                    src_weights[:, :].unsqueeze(1).to_broadcast([P, G, C]), ALU.mult))
                yield
                own.wait()
                own.mark(nc.vector.reduce_sum(e_src_sum[:, :], e_src_terms, X))
                yield
                own.wait()
                nc.vector.tensor_scalar(shift_e_src[:, bass.ds(g * G, G)], e_src_sum[:, :],
                                        (SLOPE - 1.0) / SCALE, None, ALU.mult)
                nc.vector.tensor_copy(values[:, bass.ds(g * G, G), :],
                                      ps[:, PROJ_BANK, :].rearrange("p (u c) -> p u c", c=C))\
                    .then_inc(values_ready, 1)

            def make_mask(g, s, half, first):
                if half == 0:
                    dve.wait_ge(adj_in[s], g * 16 + 16 * (GROUPS + 1))
                    if not first or s >= MASKS:
                        dve.wait_ge(mask_out[s % MASKS], g * 32 + s // MASKS * 16)
                cols = slice(half * HALF, (half + 1) * HALF)
                made = nc.vector.tensor_scalar(mask[:, s % MASKS, cols], work[:, s, cols], 0.0, MASKED,
                                               ALU.is_le, ALU.mult)
                if half == 1:
                    made.then_inc(mask_made[s % MASKS], 1)

            def back_group(g, par, first=False):
                finish = iter(()) if first else finish_back(g - 1, 1 - par)
                for k in range(TILES):
                    dve.wait_ge(adjT_high_made, g * TILES + k + 1)
                    low_part(adjT_low[:, k % 4, :], ps[:, k % 4, :], adjT_high[:, k % 4, :])\
                        .then_inc(adjT_low_made, 1)
                    if first and k in (3, 6, 10):
                        filter_bank(5 + (3, 6, 10).index(k))
                    if first and k % 4 == 2 and k < TILES - 4:
                        filtered_low_part(k // 4 + 1)
                    if k in FINISH_STEPS:
                        next(finish, None)
                    if k in MASK_STEPS:
                        n = MASK_STEPS.index(k)
                        make_mask(g, n // 2, n % 2, first)

            FINISH_STEPS = (2, 6, 7, 8, 17, 20, 24, 25, 26)
            MASK_STEPS = (0, 4, 10, 13, 18, 22, 28, 30)
            back_group(0, 0, True)
            back_group(1, 1)
            with dve.Fori(1, GROUPS // 2) as j:
                own.enter_loop(j - 1, 2 * 4)
                back_group(j * 2, 0)
                back_group(j * 2 + 1, 1)
                own.leave_loop(GROUPS // 2 - 1)

            READY = [slice(0, HALF), slice(HALF, N - GW)]
            LAST = slice(N - GW, N)

            def lift(n, slot, u, cols):
                return nc.vector.scalar_tensor_tensor(
                    row_buffer[slot][u][:, cols], slope_e_dst[:, cols],
                    shift_e_src[:, bass.ds(n * PAIR + u, 1)], e_dst[:, cols], ALU.add, ALU.max)

            def open_diagonal(n, u):
                dve.wait_ge(mask_back[u], n * 16 + 16)
                diagonal = mask[:, u, bass.ds(n * PW + u * P, P)]
                nc.vector.tensor_tensor(diagonal, diagonal, not_ident[:, :], ALU.mult).then_inc(opened, 1)

            def score(slot, u, h, cols, so_far=-3.0e38):
                rows = row_buffer[slot][u][:, cols]
                return nc.vector.tensor_tensor_reduce(
                    out=rows, in0=rows, in1=mask[:, u, cols],
                    scale=SCALE, scalar=so_far, op0=ALU.add, op1=ALU.max,
                    accum_out=part_max[:, u, h:h + 1])

            def lift_half(n, slot, u, h):
                lift(n, slot, u, slice(h * HALF, (h + 1) * HALF)).then_inc(lifted, 1)

            def score_half(n, slot, u, h):
                dve.wait_ge(lifted, n * 2 * PAIR + 2 * u + h + 1)
                if h == 0:
                    dve.wait_ge(opened, n * PAIR + u + 1)
                nc.vector.nop().then_inc(seen_vector, 1)
                score(slot, u, h, slice(h * HALF, (h + 1) * HALF)).then_inc(scores_ready, 1)

            def negate_max(n, slot, u):
                dve.wait_ge(scores_ready, n * 2 * PAIR + 2 * u + 2)
                nc.vector.tensor_scalar(minus_max[:, slot, u:u + 1], part_max[:, u, 0:1],
                                        part_max[:, u, 1:2], -1.0, ALU.max, ALU.mult).then_inc(max_ready, 1)

            def score_pair(n, slot, first_ring=False, finish=()):
                finish = iter(finish)
                if not first_ring:
                    dve.wait_ge(probT_psum, (n - (RING - 1)) * STEPS)
                lift_half(n, slot, 0, 0)
                open_diagonal(n, 0)
                lift_half(n, slot, 0, 1)
                score_half(n, slot, 0, 0)
                lift_half(n, slot, 1, 0)
                score_half(n, slot, 0, 1)
                next(finish, None)
                negate_max(n, slot, 0)
                open_diagonal(n, 1)
                lift_half(n, slot, 1, 1)
                next(finish, None)
                score_half(n, slot, 1, 0)
                next(finish, None)
                score_half(n, slot, 1, 1)
                next(finish, None)
                negate_max(n, slot, 1)
                for _ in finish:
                    pass

            def score_first_pair():
                dve.wait_ge(adjT_psum, GROUPS * TILES)
                dve.wait_ge(values_ready, GROUPS - 1)
                finish = finish_back(GROUPS - 1, 1)
                own.then_wait(lift(0, 0, 0, READY[0]))
                next(finish)
                own.then_wait(lift(0, 0, 0, READY[1]))
                for _ in range(3):
                    next(finish)
                for cols in READY:
                    own.mark(lift(0, 0, 1, cols))
                for u in range(PAIR):
                    open_diagonal(0, u)
                dve.wait_ge(opened, PAIR)
                for h in range(2):
                    own.then_wait(score(0, 0, h, READY[h]))
                    next(finish)
                dve.wait_ge(dst_ready, GROUPS)
                for u in range(PAIR):
                    lift(0, 0, u, LAST).then_inc(lifted, 2)
                dve.wait_ge(lifted, 2)
                score(0, 0, 1, LAST, part_max[:, 0, 1:2]).then_inc(scores_ready, 2)
                negate_max(0, 0, 0)
                dve.wait_ge(lifted, 4)
                for h in range(2):
                    score(0, 1, h, slice(h * HALF, (h + 1) * HALF)).then_inc(scores_ready, 1)
                negate_max(0, 0, 1)
                for _ in finish:
                    pass

            def finish_attention(n, slot):
                dve.wait_ge(rows_psum, n + (GROUPS + 1))
                dve.wait_ge(x1g_in, n * 16 + 16)
                dve.wait_ge(x1_ready, n + GROUPS)
                own.mark(nc.vector.reduce_sum(row_sum[:, :], part_sum[:, slot, :, :], X))
                yield
                own.wait()
                own.mark(nc.vector.reciprocal(one_over_sum[:, :], row_sum[:, :]))
                yield
                own.wait()
                for u in range(PAIR):
                    last = nc.vector.scalar_tensor_tensor(
                        x_rows[:, u, :], ps[:, ROWS_BANK, u * C:(u + 1) * C], one_over_sum[:, u:u + 1],
                        x_rows[:, u, :], ALU.mult, ALU.add)
                last.then_inc(x1g_added, 1)
                yield
                dve.wait_ge(x1g_added, n + 1)
                yield from statistics(PAIR)

            score_first_pair()
            score_pair(1, 1, True)
            for n in range(2, RING):
                score_pair(n, n, True, finish_attention(n - 2, n - 2))
            with dve.Fori(1, PAIRS // RING) as j:
                own.enter_loop(j - 1, RING * 4)
                for slot in range(RING):
                    n = j * RING + slot
                    score_pair(n, slot, False, finish_attention(n - 2, (slot - 2) % RING))
                own.leave_loop(PAIRS // RING - 1)
            for n in (PAIRS - 2, PAIRS - 1):
                for _ in finish_attention(n, n % RING):
                    pass


_INS = ['x', 'adj', 'L0_gnn_evals', 'L0_gnn_t', 'L1_gnn_W', 'L1_gnn_a']


def kernel(**inputs):
    import numpy as _np
    import concourse.bacc as _bacc
    from concourse import mybir as _mybir
    from concourse.bass_utils import run_bass_kernel_spmd as _run

    nc = _bacc.Bacc("TRN2", target_bir_lowering=False, num_devices=1)
    arrays, args = {}, []
    for name in _INS:
        arr = _np.ascontiguousarray(inputs[name])
        arrays[f"in_{name}"] = arr
        args.append(nc.dram_tensor(f"in_{name}", arr.shape, _mybir.dt.from_np(arr.dtype),
                                   kind="ExternalInput").ap())
    out = nc.dram_tensor("out", inputs['x'].shape, _mybir.dt.float32, kind="ExternalOutput").ap()
    build(nc, *args, out)
    return _run(nc, [arrays], core_ids=[0]).results[0]["out"]
```

```python
from contextlib import ExitStack

import concourse.bass as bass
from concourse import mybir


class StepCount:

    def __init__(self, engine, sem):
        self.engine, self.sem, self.base, self.steps = engine, sem, 0, 0

    def mark(self, instruction):
        self.steps += 1
        instruction.then_inc(self.sem, 1)

    def wait(self):
        self.engine.wait_ge(self.sem, self.base + self.steps)

    def then_wait(self, instruction):
        self.mark(instruction)
        self.wait()

    def enter_loop(self, turn, per_turn):
        self.outside = self.base + self.steps
        self.per_turn = per_turn
        self.base, self.steps = turn * per_turn + self.outside, 0

    def leave_loop(self, turns):
        assert self.steps == self.per_turn, self.steps
        self.base, self.steps = self.outside + turns * self.per_turn, 0


def build(nc, x, adj, evals, t, W, a, out):
    fp32 = mybir.dt.float32
    fp32r = mybir.dt.float32r
    int8 = mybir.dt.int8
    ALU = mybir.AluOpType
    ACT = mybir.ActivationFunctionType
    X = mybir.AxisListType.X

    N, C = x.shape
    P = 128
    TILES = N // P
    G = 4
    GW = G * P
    GROUPS = N // GW
    SLOTS = 4
    MASKS = 2
    PAIR = 2
    PW = PAIR * P
    PAIRS = N // PW
    STEPS = TILES // PAIR
    RING = 4
    PIECE = N // SLOTS
    KP = PIECE // P
    BANKS = 8
    VECTOR_BANKS, SCALAR_BANKS = (0, 2, 4), (1, 3, 5, 6, 7)
    LEAD = 3
    HALF = N // 2
    PARTS = 1 + SLOTS
    EPS = 1e-5
    SLOPE = 0.2
    MASKED = -128.0
    SCALE = 2.0 ** 46

    mask_dram = nc.dram_tensor("mask_dram", [N, N], int8, kind="Internal").ap()
    x1_dram = nc.dram_tensor("x1_dram", [N, C], fp32, kind="Internal").ap()

    def rows_of_group(ap, g):
        return ap[bass.ds(g * GW, GW), :].rearrange("(u p) c -> p u c", p=P)

    def rows_of_pair(ap, n):
        return ap[bass.ds(n * PW, PW), :].rearrange("(u p) c -> p u c", p=P)

    with ExitStack() as ctx:
        def sb(name, shape, dt=fp32):
            return ctx.enter_context(nc.sbuf_tensor(name, shape, dt))

        def sem(name):
            return ctx.enter_context(nc.semaphore(name))

        work = sb("work", [P, SLOTS, N])
        with ExitStack() as products:
            def parts(name, shape):
                return products.enter_context(nc.sbuf_tensor(name, shape, fp32r))

            adjT_high, adjT_low = parts("adjT_high", [P, 4, GW]), parts("adjT_low", [P, 4, GW])
            split_high, split_low = parts("split_high", [P, N]), parts("split_low", [P, N])
        late_rows = sb("late_rows", [P, 4, N])
        spectrumT = late_rows[:, 0, :]
        filtered = late_rows[:, 3, :].rearrange("p (k c) -> p k c", c=C)
        turned = sb("turned", [P, 4, GW])

        def piece_parts(q):
            return split_high[:, q * PIECE:(q + 1) * PIECE], split_low[:, q * PIECE:(q + 1) * PIECE]

        x_high = adjT_high[:, 0, :].rearrange("p (s c) -> p s c", c=C)
        x_low = adjT_low[:, 0, :].rearrange("p (s c) -> p s c", c=C)
        filtered_high = split_high[:, :].rearrange("p (k c) -> p k c", c=C)
        filtered_low = split_low[:, :].rearrange("p (k c) -> p k c", c=C)
        row_buffer = [[work[:, 0, :], work[:, 1, :]], [work[:, 2, :], work[:, 3, :]],
                      [late_rows[:, 0, :], late_rows[:, 1, :]], [late_rows[:, 2, :], late_rows[:, 3, :]]]
        mask = sb("mask", [P, MASKS, N], int8)
        values = sb("values", [P, TILES, C])
        e_dst = sb("e_dst", [P, N])
        slope_e_dst = sb("slope_e_dst", [P, N])
        x_rows = sb("x_rows", [P, G, C])
        sumT = sb("sumT", [P, GW])
        x1_rows = sb("x1_rows", [P, G, C])
        x1T = sumT
        e_src_terms = sumT[:, :].rearrange("p (u c) -> p u c", c=C)
        ALL = slice(0, G)
        TWO = [slice(0, PAIR), slice(PAIR, 2 * PAIR)]
        ident = sb("ident", [P, P])
        not_ident = sb("not_ident", [P, P], int8)
        w_sb = sb("w_sb", [P, C])
        wT = late_rows[:, 3, 0:C]
        a_sb = late_rows[0:2, 3, C:2 * C]
        aT = late_rows[:, 3, 2 * C:2 * C + 2]
        a_wide = late_rows[:, 3, 3 * C:5 * C].rearrange("p (j q) -> p j q", j=2)
        evals_sb = late_rows[0:TILES, 3, 5 * C:6 * C]
        ones = late_rows[0:1, 3, 6 * C:7 * C]
        src_weights = sb("src_weights", [P, C])
        dst_weights = sb("dst_weights", [P, P])
        t_sb = sb("t_sb", [1, 1])
        minus_t = sb("minus_t", [P, 1])
        coefs = sb("coefs", [P, TILES])
        stats = sb("stats", [P, G, 6])
        mean_var = sb("mean_var", [P, G, 2])
        minus_mean, var, rstd, half = (sb(n, [P, G]) for n in ("minus_mean", "var", "rstd", "half"))
        shift_e_src = sb("shift_e_src", [P, TILES])
        part_max = sb("part_max", [P, PAIR, 2])
        minus_max = sb("minus_max", [P, RING, PAIR])
        part_sum = sb("part_sum", [P, RING, PAIR, 2])
        row_sum = sb("row_sum", [P, PAIR])
        one_over_sum = sb("one_over_sum", [P, PAIR])
        e_src_sum = sb("e_src_sum", [P, G])

        ps = ctx.enter_context(nc.psum_tensor("ps", [P, BANKS, 512], fp32))
        ROWS_BANK, PROJ_BANK = 6, 7

        consts_in = sem("consts_in")
        ident_made = sem("ident_made")
        own_gpsimd = sem("own_gpsimd")
        own_vector = sem("own_vector")
        seen_gpsimd = sem("seen_gpsimd")
        seen_vector = sem("seen_vector")
        seen_sync = sem("seen_sync")
        setup_turned = sem("setup_turned")
        setup_copied = sem("setup_copied")
        setup_weights = sem("setup_weights")
        setup_done = sem("setup_done")
        coefs_made = sem("coefs_made")
        adj_in = [sem(f"adj_in{s}") for s in range(SLOTS)]
        adj_right_in = [sem(f"adj_right_in{s}") for s in range(SLOTS)]
        x_in = [sem(f"x_in{s}") for s in range(SLOTS)]
        high_made = sem("high_made")
        low_made = sem("low_made")
        pieces_used = sem("pieces_used")
        mask_made = [sem(f"mask_made{s}") for s in range(MASKS)]
        mask_out = [sem(f"mask_out{s}") for s in range(MASKS)]
        spectrum_vector = sem("spectrum_vector")
        spectrum_scalar = sem("spectrum_scalar")
        spectrum_rows = sem("spectrum_rows")
        filtered_made = sem("filtered_made")
        filtered_high_made = sem("filtered_high_made")
        filtered_low_made = sem("filtered_low_made")
        adjT_psum = sem("adjT_psum")
        adjT_high_made = sem("adjT_high_made")
        adjT_low_made = sem("adjT_low_made")
        adjT_used = sem("adjT_used")
        xg_in = sem("xg_in")
        rows_added = sem("rows_added")
        sumT_ready = sem("sumT_ready")
        rows_psum = sem("rows_psum")
        var_ready = sem("var_ready")
        rstd_ready = sem("rstd_ready")
        centred = sem("centred")
        x1_ready = sem("x1_ready")
        x1_out = sem("x1_out")
        x1T_psum = sem("x1T_psum")
        x1T_ready = sem("x1T_ready")
        values_psum = sem("values_psum")
        values_ready = sem("values_ready")
        dst_psum = sem("dst_psum")
        dst_ready = sem("dst_ready")
        e_src_ready = sem("e_src_ready")
        mask_back = [sem(f"mask_back{s}") for s in range(MASKS)]
        opened = sem("opened")
        lifted = sem("lifted")
        scores_ready = sem("scores_ready")
        max_ready = sem("max_ready")
        probs_ready = sem("probs_ready")
        probT_psum = sem("probT_psum")
        probT_ready = sem("probT_ready")
        probT_used = sem("probT_used")
        x1g_in = [sem(f"x1g_in{i}") for i in range(2)]
        x1g_added = sem("x1g_added")
        last_out = sem("last_out")
        y_out = [sem(f"y_out{i}") for i in range(2)]

        block = ctx.enter_context(nc.Block())

        @block.sync
        def _(sp):
            def load_tiles(g, first):
                for s in range(SLOTS):
                    if not first:
                        sp.wait_ge(low_made, g * (SLOTS * PARTS) + PARTS * (s + 1 - SLOTS))
                    sp.dma_start(x_rows[:, s, :], x[bass.ds(g * GW + s * P, P), :]).then_inc(x_in[s], 16)
                    for cols, landed in ((slice(0, HALF), adj_in[s]), (slice(HALF, N), adj_right_in[s])):
                        sp.dma_start(work[:, s, cols], adj[bass.ds(g * GW + s * P, P), cols]).then_inc(landed, 16)

            load_tiles(0, True)
            with sp.Fori(1, GROUPS) as g:
                load_tiles(g, False)

            def load_piece(g, s):
                sp.dma_start(work[:, s, :].rearrange("p (u k) -> p u k", u=G),
                             rows_of_group(adj, g)[:, :, s * PIECE:(s + 1) * PIECE])\
                    .then_inc(adj_in[s], 16)

            def write_mask(g, s):
                sp.wait_ge(mask_made[s % MASKS], g * 2 + (s // MASKS + 1))
                nc.sync.nop().then_inc(seen_sync, 1)
                sp.dma_start(rows_of_group(mask_dram, g)[:, :, s * PIECE:(s + 1) * PIECE],
                             mask[:, s % MASKS, :].rearrange("p (u k) -> p u k", u=G))\
                    .then_inc(mask_out[s % MASKS], 16)

            def load_x(g):
                sp.dma_start(x_rows[:, :, :], rows_of_group(x, g)).then_inc(xg_in, 16)

            for s in range(SLOTS):
                sp.wait_ge(low_made, PARTS * (TILES - SLOTS + s + 1))
                load_piece(0, s)
            load_x(0)

            def pass_group(g, first):
                for s in range(SLOTS):
                    sp.wait_ge(adjT_psum, g * TILES + (s + 1) * KP)
                    nc.sync.nop().then_inc(seen_sync, 1)
                    write_mask(g, s)
                    load_piece(g + 1, s)
                    if s == 1 and not first:
                        sp.wait_ge(x1_ready, g)
                        nc.sync.nop().then_inc(seen_sync, 1)
                        load_x(g)

            pass_group(0, True)
            with sp.Fori(1, GROUPS - 1) as g:
                pass_group(g, False)
            for s in range(SLOTS):
                write_mask(GROUPS - 1, s)
                if s == 1:
                    sp.wait_ge(x1_ready, GROUPS - 1)
                    load_x(GROUPS - 1)

            for s in range(MASKS):
                sp.wait_ge(mask_out[s], 2 * 16 * GROUPS)

            def load_mask(n, first):
                for u in range(PAIR):
                    if not first:
                        sp.wait_ge(scores_ready, n * 2 * PAIR + (2 * u + 2 - 2 * PAIR))
                    sp.dma_start(mask[:, u, :], mask_dram[bass.ds(n * PW + u * P, P), :])\
                        .then_inc(mask_back[u], 16)

            load_mask(0, True)
            with sp.Fori(1, PAIRS) as n:
                load_mask(n, False)

            sp.wait_ge(x1_ready, GROUPS + PAIRS)
            sp.dma_start(rows_of_pair(out, PAIRS - 1), x1_rows[:, TWO[1], :]).then_inc(last_out, 16)
            sp.wait_ge(last_out, 16)

        @block.gpsimd
        def _(pool):
            nc.gpsimd.memset(ident[:, :], 0.0).then_inc(own_gpsimd, 1)
            nc.gpsimd.memset(not_ident[:, :], 1.0).then_inc(own_gpsimd, 1)
            nc.gpsimd.memset(ones[:, :], 1.0).then_inc(own_gpsimd, 1)
            nc.gpsimd.memset(half[:, :], -0.5).then_inc(own_gpsimd, 1)
            pool.wait_ge(own_gpsimd, 4)
            for m, fill in ((ident, 1.0), (not_ident, 0.0)):
                nc.gpsimd.affine_select(out=m[:, :], in_=m[:, :], compare_op=ALU.not_equal, fill=fill,
                                        base=0, pattern=[[-1, P]], channel_multiplier=1)\
                    .then_inc(ident_made, 1)

            def invert(turn, us):
                pool.wait_ge(var_ready, turn + 1)
                nc.gpsimd.tensor_tensor(rstd[:, us], var[:, us], half[:, us], ALU.pow)\
                    .then_inc(rstd_ready, 1)

            with pool.Fori(0, GROUPS) as g:
                invert(g, ALL)
                pool.wait_ge(x1_ready, g + 1)
                nc.gpsimd.nop().then_inc(seen_gpsimd, 1)
                pool.dma_start(rows_of_group(x1_dram, g), x1_rows[:, :, :]).then_inc(x1_out, 16)
            pool.wait_ge(x1_out, 16 * GROUPS)

            def load_x1(n, i):
                pool.dma_start(x_rows[:, TWO[i], :], rows_of_pair(x1_dram, n)).then_inc(x1g_in[i], 16)

            def write_rows(n, i):
                invert(n + GROUPS, TWO[i])
                pool.wait_ge(x1_ready, n + (GROUPS + 1))
                nc.gpsimd.nop().then_inc(seen_gpsimd, 1)
                pool.dma_start(rows_of_pair(out, n), x1_rows[:, TWO[i], :]).then_inc(y_out[i], 16)

            for i in range(2):
                load_x1(i, i)
            with pool.Fori(0, PAIRS // 2 - 1) as j:
                for i in range(2):
                    write_rows(j * 2 + i, i)
                    load_x1(j * 2 + (i + 2), i)
            write_rows(PAIRS - 2, 0)
            pool.wait_ge(y_out[0], 16 * (PAIRS // 2))
            pool.wait_ge(y_out[1], 16 * (PAIRS // 2 - 1))
            invert(PAIRS - 1 + GROUPS, TWO[1])

        @block.tensor
        def _(pe):
            pe.wait_ge(ident_made, 2)
            pe.wait_ge(consts_in, 64)
            nc.tensor.transpose(ps[:, 0, 0:TILES], evals_sb[:, :], ident[0:TILES, 0:TILES])
            nc.tensor.transpose(ps[:, 1, 0:C], w_sb[:, :], ident[:, :])
            nc.tensor.transpose(ps[:, 2, 0:2], a_sb[:, :], ident[0:2, 0:2])
            nc.tensor.matmul(ps[:, 3, 0:1], ones[:, :], t_sb[:, :], start=True, stop=True)\
                .then_inc(setup_turned, 1)
            pe.wait_ge(setup_copied, 1)
            nc.tensor.matmul(ps[:, 4, 0:C], a_wide[:, 0, :], wT[:, :], start=True, stop=True)
            nc.tensor.matmul(ps[:, 5, 0:P], wT[:, :], a_wide[:, 1, :], start=True, stop=True)\
                .then_inc(setup_weights, 1)
            pe.wait_ge(setup_done, 1)
            pe.wait_ge(coefs_made, 1)

            def spectral(g, first=False, last=False):
                for s in range(SLOTS):
                    for q in range(SLOTS):
                        pe.wait_ge(low_made, g * (SLOTS * PARTS) + s * PARTS + q + 2)
                        high, low = piece_parts(q)
                        for b in range(2):
                            cols = slice(b * 512, (b + 1) * 512)
                            for n, (xs, adjs) in enumerate(((x_high, high), (x_low, high), (x_high, low))):
                                mm = nc.tensor.matmul(ps[:, 2 * q + b, :], xs[:, s, :], adjs[:, cols],
                                                      start=(first and s == 0 and n == 0),
                                                      stop=(last and s == SLOTS - 1 and n == 2))
                        mm.then_inc(pieces_used, 1)

            spectral(0, first=True)
            with pe.Fori(1, GROUPS - 1) as g:
                spectral(g)
            spectral(GROUPS - 1, last=True)

            for b in range(BANKS):
                if b in VECTOR_BANKS:
                    pe.wait_ge(spectrum_vector, VECTOR_BANKS.index(b) + 1)
                else:
                    pe.wait_ge(spectrum_scalar, SCALAR_BANKS.index(b) + 1)
                for u in range(G):
                    mm = nc.tensor.transpose(ps[:, b, u * P:(u + 1) * P],
                                             spectrumT[:, b * 512 + u * P:b * 512 + (u + 1) * P], ident[:, :])
                mm.then_inc(spectrum_rows, 1)

            def back_product(g, m, par, first, first_pair):
                pe.wait_ge(adjT_low_made, g * TILES + m + 1)
                if m == 0 and not first_pair:
                    pe.wait_ge(sumT_ready, g - 1)
                if first and m == 0:
                    pe.wait_ge(filtered_made, 4 + 1)
                if first and m % G == 0:
                    pe.wait_ge(filtered_low_made, m // G + 1)
                for n, (ys, adjs) in enumerate(((filtered_high, adjT_high[:, m % 4, :]),
                                                (filtered_low, adjT_high[:, m % 4, :]),
                                                (filtered_high, adjT_low[:, m % 4, :]))):
                    mm = nc.tensor.matmul(ps[:, 4 + par, :], ys[:, m, :], adjs,
                                          start=(m == 0 and n == 0), stop=(m == TILES - 1 and n == 2))
                mm.then_inc(adjT_used, 1)

            def project(g, k):
                if k == 5:
                    pe.wait_ge(sumT_ready, g + 1)
                    for u in range(G):
                        mm = nc.tensor.transpose(ps[:, ROWS_BANK, u * P:(u + 1) * P],
                                                 sumT[:, u * P:(u + 1) * P], ident[:, :])
                    mm.then_inc(rows_psum, 1)
                if k == 16:
                    pe.wait_ge(x1_ready, g + 1)
                    for u in range(G):
                        mm = nc.tensor.transpose(ps[:, ROWS_BANK, u * P:(u + 1) * P],
                                                 x1_rows[:, u, :], ident[:, :])
                    mm.then_inc(x1T_psum, 1)
                if k == 19:
                    pe.wait_ge(x1T_ready, g + 1)
                    nc.tensor.matmul(ps[:, PROJ_BANK, :], dst_weights[:, :], x1T[:, :],
                                     start=True, stop=True).then_inc(dst_psum, 1)
                if k == 23:
                    pe.wait_ge(dst_ready, g + 1)
                    for u in range(G):
                        mm = nc.tensor.matmul(ps[:, PROJ_BANK, u * C:(u + 1) * C],
                                              x1T[:, u * P:(u + 1) * P], w_sb[:, :], start=True, stop=True)
                    mm.then_inc(values_psum, 1)

            def back_group(g, par, first_pair=False):
                first = first_pair and par == 0
                for k in range(TILES):
                    s = k // KP
                    if k % KP == 0:
                        pe.wait_ge(adj_in[s], g * 16 + 16 * (GROUPS + 1))
                    if first and k < LEAD + 1:
                        pe.wait_ge(filtered_made, k + 1)
                    for u in range(G):
                        c = u * PIECE + (k % KP) * P
                        mm = nc.tensor.transpose(ps[:, k % 4, u * P:(u + 1) * P],
                                                 work[:, s, c:c + P], ident[:, :])
                    mm.then_inc(adjT_psum, 1)
                    if k >= LEAD:
                        back_product(g, k - LEAD, par, first, first_pair)
                    elif not first:
                        back_product(g - 1, k - LEAD + TILES, 1 - par, False, False)
                    if not first:
                        project(g - 1, k)

            back_group(0, 0, True)
            back_group(1, 1, True)
            with pe.Fori(1, GROUPS // 2) as j:
                back_group(j * 2, 0)
                back_group(j * 2 + 1, 1)
            for m in range(TILES - LEAD, TILES):
                back_product(GROUPS - 1, m, 1, False, False)
            for k in (5, 16, 19, 23):
                project(GROUPS - 1, k)

            def attend(n, slot, k, first_pairs=False, first_group=False):
                pe.wait_ge(probT_ready, n * STEPS + k + 1)
                if first_group and k == (TILES - G) // 2:
                    pe.wait_ge(values_ready, GROUPS)
                if k == 0 and not first_pairs:
                    pe.wait_ge(sumT_ready, n + (GROUPS - 1))
                for i in range(2):
                    mm = nc.tensor.matmul(ps[:, 4 + slot % 2, :PW], values[:, 2 * k + i, :],
                                          turned[:, k % 4, i * PW:(i + 1) * PW],
                                          start=(k == 0 and i == 0), stop=(k == STEPS - 1 and i == 1))
                mm.then_inc(probT_used, 1)

            def attended_rows(n, first=False):
                pe.wait_ge(sumT_ready, n + (GROUPS + 1))
                if not first:
                    pe.wait_ge(x1g_added, n)
                for u in range(PAIR):
                    mm = nc.tensor.transpose(ps[:, ROWS_BANK, u * P:(u + 1) * P],
                                             sumT[:, u * P:(u + 1) * P], ident[:, :])
                mm.then_inc(rows_psum, 1)

            def attend_pair(n, slot, first=False, second=False):
                for k in range(STEPS):
                    if k == 0:
                        pe.wait_ge(probs_ready, n * 2 * PAIR + 2 * PAIR - (2 if first else 1))
                    if k == STEPS // 2:
                        pe.wait_ge(probs_ready, n * 2 * PAIR + 2 * PAIR)
                    for i in range(2):
                        for u in range(PAIR):
                            m = 2 * k + i
                            mm = nc.tensor.transpose(ps[:, k % 4, i * PW + u * P:i * PW + (u + 1) * P],
                                                     row_buffer[slot][u][:, m * P:(m + 1) * P], ident[:, :])
                    mm.then_inc(probT_psum, 1)
                    if k >= LEAD:
                        attend(n, slot, k - LEAD, first or second, first)
                    elif not first:
                        attend(n - 1, (slot - 1) % RING, k - LEAD + STEPS, second)
                    if k == 5 and not first:
                        attended_rows(n - 1, second)

            pe.wait_ge(values_ready, GROUPS - 1)
            for n in range(RING):
                attend_pair(n, n, first=(n == 0), second=(n == 1))
            with pe.Fori(1, PAIRS // RING) as j:
                for slot in range(RING):
                    attend_pair(j * RING + slot, slot)
            for k in range(STEPS - LEAD, STEPS):
                attend(PAIRS - 1, RING - 1, k)
            attended_rows(PAIRS - 1)

        @block.scalar
        def _(act):
            act.dma_start(w_sb[:, :], W).then_inc(consts_in, 16)
            act.dma_start(a_sb[:, :], a.rearrange("(j d) -> j d", j=2)).then_inc(consts_in, 16)
            act.dma_start(evals_sb[:, :], evals.rearrange("(k p) -> k p", p=P)).then_inc(consts_in, 16)
            act.dma_start(t_sb[:, :], t.rearrange("(a b) -> a b", a=1)).then_inc(consts_in, 16)

            act.wait_ge(setup_copied, 1)
            nc.scalar.activation(coefs[:, :], ps[:, 0, 0:TILES], ACT.Exp, scale=minus_t[:, 0:1])\
                .then_inc(coefs_made, 1)

            def split_high_parts(g, first):
                for s in range(SLOTS):
                    act.wait_ge(x_in[s], g * 16 + 16)
                    if not first:
                        act.wait_ge(pieces_used, g * (SLOTS * SLOTS) + (s + 1 - SLOTS) * SLOTS)
                    nc.scalar.activation(x_high[:, s, :], x_rows[:, s, :], ACT.Copy).then_inc(high_made, 1)
                    for q in range(SLOTS):
                        if q == 0:
                            act.wait_ge(adj_in[s], g * 16 + 16)
                        if q == SLOTS // 2:
                            act.wait_ge(adj_right_in[s], g * 16 + 16)
                        if not first or s > 0:
                            act.wait_ge(pieces_used, g * (SLOTS * SLOTS) + (s - 1) * SLOTS + q + 1)
                        nc.scalar.activation(piece_parts(q)[0], work[:, s, q * PIECE:(q + 1) * PIECE], ACT.Copy)\
                            .then_inc(high_made, 1)

            split_high_parts(0, True)
            with act.Fori(1, GROUPS) as g:
                split_high_parts(g, False)

            act.wait_ge(pieces_used, TILES * SLOTS)
            for b in SCALAR_BANKS:
                nc.scalar.activation(spectrumT[:, b * 512:(b + 1) * 512], ps[:, b, :], ACT.Copy)\
                    .then_inc(spectrum_scalar, 1)

            def split_filtered(b):
                act.wait_ge(filtered_made, b + 1)
                nc.scalar.activation(filtered_high[:, b * G:(b + 1) * G, :], filtered[:, b * G:(b + 1) * G, :],
                                     ACT.Copy).then_inc(filtered_high_made, 1)

            split_filtered(0)

            def centre(turn, us, out_sem, out_count):
                act.wait_ge(var_ready, turn + 1)
                if out_sem is not None:
                    act.wait_ge(out_sem, out_count)
                for u in range(us.start, us.stop):
                    last = nc.scalar.activation(x1_rows[:, u, :], x_rows[:, u, :], ACT.Identity,
                                                bias=minus_mean[:, u:u + 1])
                last.then_inc(centred, 1)

            def scale_rows(turn, us):
                act.wait_ge(centred, turn + 1)
                act.wait_ge(rstd_ready, turn + 1)
                for u in range(us.start, us.stop):
                    last = nc.scalar.activation(x1_rows[:, u, :], x1_rows[:, u, :], ACT.Copy,
                                                scale=rstd[:, u:u + 1])
                last.then_inc(x1_ready, 1)

            def finish(g, par, k, first_finish=False):
                if k == 3:
                    act.wait_ge(adjT_used, g * TILES + TILES)
                    nc.scalar.activation(sumT[:, :], ps[:, 4 + par, :], ACT.Copy).then_inc(sumT_ready, 1)
                if k == 11:
                    centre(g, ALL, None if first_finish else x1_out, g * 16)
                if k == 13:
                    scale_rows(g, ALL)
                if k == 17:
                    act.wait_ge(x1T_psum, g + 1)
                    nc.scalar.activation(x1T[:, :], ps[:, ROWS_BANK, :], ACT.Copy).then_inc(x1T_ready, 1)
                if k == 20:
                    act.wait_ge(dst_psum, g + 1)
                    nc.scalar.activation(e_dst[:, bass.ds(g * GW, GW)], ps[:, PROJ_BANK, :],
                                         ACT.Copy, scale=1.0 / SCALE)
                if k == 21:
                    nc.scalar.activation(slope_e_dst[:, bass.ds(g * GW, GW)], ps[:, PROJ_BANK, :],
                                         ACT.Copy, scale=SLOPE / SCALE).then_inc(dst_ready, 1)
                if k == 25:
                    act.wait_ge(values_psum, g + 1)
                    nc.scalar.activation(values[:, bass.ds(g * G, G), :],
                                         ps[:, PROJ_BANK, :].rearrange("p (u c) -> p u c", c=C), ACT.Copy)\
                        .then_inc(values_ready, 1)

            def split_adjT(g, par, first=False, second=False):
                for k in range(TILES):
                    act.wait_ge(adjT_psum, g * TILES + k + 1)
                    if first and k == 0:
                        act.wait_ge(spectrum_rows, BANKS)
                    if k >= 4 or not first:
                        act.wait_ge(adjT_used, g * TILES + k - 3)
                    nc.scalar.activation(adjT_high[:, k % 4, :], ps[:, k % 4, :], ACT.Copy)\
                        .then_inc(adjT_high_made, 1)
                    if first and k % 4 == 1 and k < TILES - 4:
                        split_filtered(k // 4 + 1)
                    if not first:
                        finish(g - 1, 1 - par, k, second)

            split_adjT(0, 0, first=True)
            split_adjT(1, 1, second=True)
            with act.Fori(1, GROUPS // 2) as j:
                split_adjT(j * 2, 0)
                split_adjT(j * 2 + 1, 1)
            for k in range(TILES):
                finish(GROUPS - 1, 1, k)

            def exponent(n, slot, u, h):
                act.wait_ge(max_ready, n * PAIR + u + 1)
                rows = row_buffer[slot][u][:, h * HALF:(h + 1) * HALF]
                nc.scalar.activation(rows, rows, ACT.Exp, bias=minus_max[:, slot, u:u + 1],
                                     accum_out=part_sum[:, slot, u, h:h + 1]).then_inc(probs_ready, 1)

            def copy_sumT(n, slot):
                act.wait_ge(probT_used, n * STEPS + STEPS)
                nc.scalar.activation(sumT[:, :PW], ps[:, 4 + slot % 2, :PW], ACT.Copy).then_inc(sumT_ready, 1)

            def write_rows(n, slot, first_pairs=False):
                i = slot % 2
                if first_pairs:
                    centre(n + GROUPS, TWO[i], x1_out, GROUPS * 16)
                else:
                    centre(n + GROUPS, TWO[i], y_out[i], n * 8 - i * 8)
                scale_rows(n + GROUPS, TWO[i])

            def window(n, slot, first=False, last=False, early=None):
                after = (slot + 1) % RING
                when = (8, 10, 14) if first else (5, 9, 13)
                for k in range(STEPS):
                    act.wait_ge(probT_psum, n * STEPS + k + 1)
                    if k >= 4 or not first:
                        act.wait_ge(probT_used, n * STEPS + k - 3)
                    nc.scalar.activation(turned[:, k % 4, :], ps[:, k % 4, :], ACT.Copy)\
                        .then_inc(probT_ready, 1)
                    if k == 1:
                        exponent(n, slot, 0 if first else 1, 1)
                    if k == 3 and first:
                        exponent(n, slot, 1, 1)
                    if k == 3 and not first:
                        copy_sumT(n - 1, (slot - 1) % RING)
                    if k == 4 and early not in (0, 1):
                        write_rows(n - 2, (slot - 2) % RING, early in (2, 3))
                    if k == 11 and last:
                        write_rows(n - 1, (slot - 1) % RING)
                    if k in when and not last:
                        exponent(n + 1, after, *((0, 0), (0, 1), (1, 0))[when.index(k)])

            for u in range(PAIR):
                exponent(0, 0, u, 0)
            for n in range(RING):
                window(n, n, first=(n == 0), early=n)
            with act.Fori(1, PAIRS // RING - 1) as j:
                for slot in range(RING):
                    window(j * RING + slot, slot)
            for slot in range(RING):
                window(PAIRS - RING + slot, slot, last=(slot == RING - 1))
            copy_sumT(PAIRS - 1, RING - 1)
            write_rows(PAIRS - 1, RING - 1)

        @block.vector
        def _(dve):
            own = StepCount(dve, own_vector)
            dve.wait_ge(setup_turned, 1)
            own.then_wait(nc.vector.tensor_copy(aT[:, :], ps[:, 2, 0:2]))
            nc.vector.tensor_copy(wT[:, :], ps[:, 1, 0:C])
            nc.vector.tensor_scalar(minus_t[:, :], ps[:, 3, 0:1], 1e-8, -1.0, ALU.max, ALU.mult)
            for j in range(2):
                cp = nc.vector.tensor_copy(a_wide[:, j, :], aT[:, j:j + 1].to_broadcast([P, P]))
            cp.then_inc(setup_copied, 1)
            dve.wait_ge(setup_weights, 1)
            nc.vector.tensor_copy(src_weights[:, :], ps[:, 4, 0:C])
            nc.vector.tensor_copy(dst_weights[:, :], ps[:, 5, 0:P]).then_inc(setup_done, 1)
            dve.wait_ge(ident_made, 2)

            def low_part(low, whole, high):
                return nc.vector.tensor_tensor(low, whole, high.bitcast(fp32), ALU.subtract)

            def split_low_parts(g):
                for s in range(SLOTS):
                    dve.wait_ge(high_made, g * (SLOTS * PARTS) + s * PARTS + 1)
                    low_part(x_low[:, s, :], x_rows[:, s, :], x_high[:, s, :]).then_inc(low_made, 1)
                    for q in range(SLOTS):
                        dve.wait_ge(high_made, g * (SLOTS * PARTS) + s * PARTS + q + 2)
                        high, low = piece_parts(q)
                        low_part(low, work[:, s, q * PIECE:(q + 1) * PIECE], high).then_inc(low_made, 1)

            with dve.Fori(0, GROUPS) as g:
                split_low_parts(g)

            dve.wait_ge(pieces_used, TILES * SLOTS)
            for b in VECTOR_BANKS:
                nc.vector.tensor_copy(spectrumT[:, b * 512:(b + 1) * 512], ps[:, b, :])\
                    .then_inc(spectrum_vector, 1)

            def filter_bank(b):
                dve.wait_ge(spectrum_rows, b + 1)
                nc.vector.tensor_tensor(filtered[:, b * G:(b + 1) * G, :],
                                        ps[:, b, :].rearrange("p (u c) -> p u c", c=C),
                                        coefs[:, b * G:(b + 1) * G].unsqueeze(2).to_broadcast([P, G, C]),
                                        ALU.mult).then_inc(filtered_made, 1)

            def filtered_low_part(b):
                dve.wait_ge(filtered_high_made, b + 1)
                k = slice(b * G, (b + 1) * G)
                low_part(filtered_low[:, k, :], filtered[:, k, :], filtered_high[:, k, :])\
                    .then_inc(filtered_low_made, 1)

            dve.wait_ge(coefs_made, 1)
            for b in range(5):
                filter_bank(b)
            filtered_low_part(0)

            def statistics(us):
                for u in range(us.start, us.stop):
                    last = nc.vector.bn_stats(stats[:, u, :], x_rows[:, u, :])
                own.mark(last)
                yield
                own.wait()
                nc.vector.nop().then_inc(seen_vector, 1)
                for u in range(us.start, us.stop):
                    last = nc.vector.bn_aggr(mean_var[:, u, :], stats[:, u, :])
                own.mark(last)
                yield
                own.wait()
                nc.vector.tensor_scalar(minus_mean[:, us], mean_var[:, us, 0], -1.0, None, ALU.mult)
                nc.vector.tensor_scalar(var[:, us], mean_var[:, us, 1], EPS, None, ALU.add)\
                    .then_inc(var_ready, 1)

            def finish_back(g):
                dve.wait_ge(rows_psum, g + 1)
                dve.wait_ge(xg_in, g * 16 + 16)
                nc.vector.tensor_tensor(x_rows[:, :, :], ps[:, ROWS_BANK, :].rearrange("p (u c) -> p u c", c=C),
                                        x_rows[:, :, :], ALU.add).then_inc(rows_added, 1)
                yield
                dve.wait_ge(rows_added, g + 1)
                yield from statistics(ALL)
                yield
                dve.wait_ge(values_psum, g + 1)
                own.mark(nc.vector.tensor_tensor(
                    e_src_terms, x1_rows[:, :, :],
                    src_weights[:, :].unsqueeze(1).to_broadcast([P, G, C]), ALU.mult))
                yield
                own.wait()
                own.mark(nc.vector.reduce_sum(e_src_sum[:, :], e_src_terms, X))
                yield
                own.wait()
                nc.vector.tensor_scalar(shift_e_src[:, bass.ds(g * G, G)], e_src_sum[:, :],
                                        (SLOPE - 1.0) / SCALE, None, ALU.mult).then_inc(e_src_ready, 1)

            def make_mask(g, s, half, first):
                if half == 0:
                    dve.wait_ge(adj_in[s], g * 16 + 16 * (GROUPS + 1))
                    if not first or s >= MASKS:
                        dve.wait_ge(mask_out[s % MASKS], g * 32 + s // MASKS * 16)
                cols = slice(half * HALF, (half + 1) * HALF)
                made = nc.vector.tensor_scalar(mask[:, s % MASKS, cols], work[:, s, cols], 0.0, MASKED,
                                               ALU.is_le, ALU.mult)
                if half == 1:
                    made.then_inc(mask_made[s % MASKS], 1)

            def lift(n, slot, u, cols):
                return nc.vector.scalar_tensor_tensor(
                    row_buffer[slot][u][:, cols], slope_e_dst[:, cols],
                    shift_e_src[:, bass.ds(n * PAIR + u, 1)], e_dst[:, cols], ALU.add, ALU.max)

            def back_group(g, par, first=False, last=False):
                finish = iter(()) if first else finish_back(g - 1)
                for k in range(TILES):
                    dve.wait_ge(adjT_high_made, g * TILES + k + 1)
                    low_part(adjT_low[:, k % 4, :], ps[:, k % 4, :], adjT_high[:, k % 4, :])\
                        .then_inc(adjT_low_made, 1)
                    if first and k in (3, 6, 10):
                        filter_bank(5 + (3, 6, 10).index(k))
                    if first and k % 4 == 2 and k < TILES - 4:
                        filtered_low_part(k // 4 + 1)
                    if k in FINISH_STEPS:
                        next(finish, None)
                    if last and k in EARLY_STEPS:
                        dve.wait_ge(adjT_psum, g * TILES + KP)
                        dve.wait_ge(dst_ready, GROUPS - 2)
                        dve.wait_ge(e_src_ready, 1)
                        own.mark(lift(0, 0, 0, EARLY[EARLY_STEPS.index(k)]))
                    if k in MASK_STEPS:
                        n = MASK_STEPS.index(k)
                        make_mask(g, n // 2, n % 2, first)

            FINISH_STEPS = (6, 7, 8, 9, 24, 25, 26)
            MASK_STEPS = (2, 4, 11, 14, 18, 21, 27, 29)
            EARLY_STEPS = (12, 15, 22)
            EARLY = [slice(i * PIECE, (i + 1) * PIECE) for i in range(3)]
            back_group(0, 0, True)
            back_group(1, 1)
            with dve.Fori(1, GROUPS // 2 - 1) as j:
                own.enter_loop(j - 1, 2 * 4)
                back_group(j * 2, 0)
                back_group(j * 2 + 1, 1)
                own.leave_loop(GROUPS // 2 - 2)
            back_group(GROUPS - 2, 0)
            back_group(GROUPS - 1, 1, last=True)

            READY = [slice(0, HALF), slice(HALF, N - GW)]
            LAST = slice(N - GW, N)

            def open_diagonal(n, u):
                dve.wait_ge(mask_back[u], n * 16 + 16)
                diagonal = mask[:, u, bass.ds(n * PW + u * P, P)]
                nc.vector.tensor_tensor(diagonal, diagonal, not_ident[:, :], ALU.mult).then_inc(opened, 1)

            def score(slot, u, h, cols, so_far=-3.0e38):
                rows = row_buffer[slot][u][:, cols]
                return nc.vector.tensor_tensor_reduce(
                    out=rows, in0=rows, in1=mask[:, u, cols],
                    scale=SCALE, scalar=so_far, op0=ALU.add, op1=ALU.max,
                    accum_out=part_max[:, u, h:h + 1])

            def lift_half(n, slot, u, h):
                lift(n, slot, u, slice(h * HALF, (h + 1) * HALF)).then_inc(lifted, 1)

            def score_half(n, slot, u, h):
                dve.wait_ge(lifted, n * 2 * PAIR + 2 * u + h + 1)
                if h == 0:
                    dve.wait_ge(opened, n * PAIR + u + 1)
                nc.vector.nop().then_inc(seen_vector, 1)
                score(slot, u, h, slice(h * HALF, (h + 1) * HALF)).then_inc(scores_ready, 1)

            def negate_max(n, slot, u):
                dve.wait_ge(scores_ready, n * 2 * PAIR + 2 * u + 2)
                nc.vector.tensor_scalar(minus_max[:, slot, u:u + 1], part_max[:, u, 0:1],
                                        part_max[:, u, 1:2], -1.0, ALU.max, ALU.mult).then_inc(max_ready, 1)

            def score_pair(n, slot, first_ring=False, finish=()):
                finish = iter(finish)
                if not first_ring:
                    dve.wait_ge(probT_psum, (n - (RING - 1)) * STEPS)
                lift_half(n, slot, 0, 0)
                open_diagonal(n, 0)
                lift_half(n, slot, 0, 1)
                score_half(n, slot, 0, 0)
                lift_half(n, slot, 1, 0)
                score_half(n, slot, 0, 1)
                next(finish, None)
                negate_max(n, slot, 0)
                open_diagonal(n, 1)
                lift_half(n, slot, 1, 1)
                next(finish, None)
                score_half(n, slot, 1, 0)
                next(finish, None)
                score_half(n, slot, 1, 1)
                next(finish, None)
                negate_max(n, slot, 1)
                for _ in finish:
                    pass

            def score_first_pair():
                dve.wait_ge(adjT_psum, GROUPS * TILES)
                dve.wait_ge(dst_ready, GROUPS - 1)
                finish = finish_back(GROUPS - 1)
                own.mark(lift(0, 0, 0, slice(3 * PIECE, N - GW)))
                own.mark(lift(0, 0, 1, READY[0]))
                for _ in range(4):
                    next(finish)
                open_diagonal(0, 0)
                own.mark(lift(0, 0, 1, READY[1]))
                dve.wait_ge(opened, 1)
                for h in range(2):
                    own.mark(score(0, 0, h, READY[h]))
                open_diagonal(0, 1)
                dve.wait_ge(opened, 2)
                score(0, 1, 0, READY[0])
                dve.wait_ge(dst_ready, GROUPS)
                for u in range(PAIR):
                    lift(0, 0, u, LAST).then_inc(lifted, 2)
                own.wait()
                dve.wait_ge(lifted, 2)
                score(0, 0, 1, LAST, part_max[:, 0, 1:2]).then_inc(scores_ready, 2)
                negate_max(0, 0, 0)
                dve.wait_ge(lifted, 4)
                score(0, 1, 1, slice(HALF, N)).then_inc(scores_ready, 2)
                negate_max(0, 0, 1)
                for _ in finish:
                    pass

            def finish_attention(n, slot):
                dve.wait_ge(probs_ready, n * 2 * PAIR + 2 * PAIR)
                own.mark(nc.vector.reduce_sum(row_sum[:, :], part_sum[:, slot, :, :], X))
                yield
                own.wait()
                own.mark(nc.vector.reciprocal(one_over_sum[:, :], row_sum[:, :]))
                yield
                own.wait()
                dve.wait_ge(rows_psum, n + (GROUPS + 1))
                i = slot % 2
                dve.wait_ge(x1g_in[i], n * 8 - i * 8 + 16)
                for u in range(PAIR):
                    x_row = x_rows[:, i * PAIR + u, :]
                    last = nc.vector.scalar_tensor_tensor(
                        x_row, ps[:, ROWS_BANK, u * C:(u + 1) * C], one_over_sum[:, u:u + 1],
                        x_row, ALU.mult, ALU.add)
                last.then_inc(x1g_added, 1)
                yield
                dve.wait_ge(x1g_added, n + 1)
                yield from statistics(TWO[slot % 2])

            score_first_pair()
            score_pair(1, 1, True)
            for n in range(2, RING):
                score_pair(n, n, True, finish_attention(n - 2, n - 2))
            with dve.Fori(1, PAIRS // RING) as j:
                own.enter_loop(j - 1, RING * 4)
                for slot in range(RING):
                    n = j * RING + slot
                    score_pair(n, slot, False, finish_attention(n - 2, (slot - 2) % RING))
                own.leave_loop(PAIRS // RING - 1)
            for n in (PAIRS - 2, PAIRS - 1):
                for _ in finish_attention(n, n % RING):
                    pass


_INS = ['x', 'adj', 'L0_gnn_evals', 'L0_gnn_t', 'L1_gnn_W', 'L1_gnn_a']


def kernel(**inputs):
    import numpy as _np
    import concourse.bacc as _bacc
    from concourse import mybir as _mybir
    from concourse.bass_utils import run_bass_kernel_spmd as _run

    nc = _bacc.Bacc("TRN2", target_bir_lowering=False, num_devices=1)
    arrays, args = {}, []
    for name in _INS:
        arr = _np.ascontiguousarray(inputs[name])
        arrays[f"in_{name}"] = arr
        args.append(nc.dram_tensor(f"in_{name}", arr.shape, _mybir.dt.from_np(arr.dtype),
                                   kind="ExternalInput").ap())
    out = nc.dram_tensor("out", inputs['x'].shape, _mybir.dt.float32, kind="ExternalOutput").ap()
    build(nc, *args, out)
    return _run(nc, [arrays], core_ids=[0]).results[0]["out"]
```
